# Optimizing a Trainium2 kernel written in Bass

```python
import numpy as np
import jax
import jax.numpy as jnp

def _softmax(x, axis=-1):
    return jax.nn.softmax(x, axis=axis)
def _gelu(x):
    return jax.nn.gelu(x, approximate=True)
def _silu(x):
    return jax.nn.silu(x)
def _sigmoid(x):
    return jax.nn.sigmoid(x)
def _layernorm(x, axis=-1, eps=1e-5):
    m = jnp.mean(x, axis=axis, keepdims=True)
    v = jnp.var(x, axis=axis, keepdims=True)
    return (x - m) / jnp.sqrt(v + eps)
def _scatter_add(tgt, idx, src, axis=0):
    return tgt.at[idx].add(src)
def _segment_sum(src, seg, n):
    return jax.ops.segment_sum(src, seg, n)

kernel_name = 'mk_metaformer_d1_conv_nhwc256_f90abe'

def setup_inputs(seed: int = 0):
    np.random.seed(seed)
    _w = jnp.asarray
    def _rec_inputs():
        import jax
        import jax.numpy as jnp
        _gk = jax.random.key(seed)
        x = -0.0002928 + 1 * jax.random.normal(jax.random.fold_in(_gk, 1), (4, 64, 64, 256), jnp.float32)
        return x
    x = _rec_inputs()
    def _L0_conv_setup():
        import jax, jax.numpy as jnp
        import numpy as np
        BS, IH, IW, IC = (4, 64, 64, 256)
        FILTERS = 256
        KH = KW = 3
        KS = KH * KW

        def _dcnv2(x, kernel, bias, offset_kernel, offset_bias):
            bs, ih, iw, ic = x.shape
            kh, kw = (kernel.shape[0], kernel.shape[1])
            ks = kh * kw
            ph, pw = ((kh - 1) // 2, (kw - 1) // 2)
            off = jax.lax.conv_general_dilated(x, offset_kernel, window_strides=(1, 1), padding='SAME', dimension_numbers=('NHWC', 'HWIO', 'NHWC')) + offset_bias
            oyox = off[..., :2 * ks].reshape(bs, ih, iw, ks, 2)
            mask = jax.nn.sigmoid(off[..., 2 * ks:])
            yy, xx = jnp.meshgrid(jnp.arange(-ph, ph + 1), jnp.arange(-pw, pw + 1), indexing='ij')
            patch = jnp.stack([yy, xx], axis=-1).reshape(ks, 2).astype(jnp.float32)
            base = jnp.stack(jnp.meshgrid(jnp.arange(ih), jnp.arange(iw), indexing='ij'), axis=-1).astype(jnp.float32)
            phw = jnp.array([ph, pw], dtype=jnp.float32)
            gyx = base[None, :, :, None, :] + phw + patch + oyox
            bounds = jnp.array([ih + 1, iw + 1], dtype=jnp.float32)
            y0x0 = jnp.floor(gyx)
            y1x1 = jnp.clip(y0x0 + 1.0, 0.0, bounds)
            y0x0 = jnp.clip(y0x0, 0.0, bounds)
            g = jnp.clip(gyx, 0.0, bounds)
            dy0 = g[..., 0] - y0x0[..., 0]
            dx0 = g[..., 1] - y0x0[..., 1]
            dy1 = y1x1[..., 0] - g[..., 0]
            dx1 = y1x1[..., 1] - g[..., 1]
            w = jnp.stack([dy0 * dx0, dy0 * dx1, dy1 * dx0, dy1 * dx1], axis=-1)
            ys = jnp.stack([y1x1[..., 0], y1x1[..., 0], y0x0[..., 0], y0x0[..., 0]], axis=-1).astype(jnp.int32)
            xs = jnp.stack([y1x1[..., 1], y0x0[..., 1], y1x1[..., 1], y0x0[..., 1]], axis=-1).astype(jnp.int32)
            xp = jnp.pad(x, ((0, 0), (ph, ph), (pw, pw), (0, 0)))
            b = jnp.arange(bs)[:, None, None, None, None]
            samples = xp[b, ys, xs]
            bil = jnp.einsum('bhwkg,bhwkgc->bhwkc', w, samples) * mask[..., None]
            map_all = bil.reshape(bs, ih, iw, ks * ic)
            out = jnp.einsum('bhwc,cf->bhwf', map_all, kernel.reshape(ks * ic, -1)) + bias
            return out
        key = jax.random.key(seed)
        k1, k2, k3, k4, k5 = jax.random.split(key, 5)
        x = jax.random.normal(k1, (BS, IH, IW, IC), dtype=jnp.float32)
        kernel = jax.random.normal(k2, (KH, KW, IC, FILTERS), dtype=jnp.float32) * 0.02
        bias = jax.random.normal(k3, (FILTERS,), dtype=jnp.float32) * 0.02
        offset_kernel = jax.random.normal(k4, (KH, KW, IC, 3 * KS), dtype=jnp.float32) * 0.01
        offset_bias = jax.random.normal(k5, (3 * KS,), dtype=jnp.float32) * 0.01
        return {'x': x, 'kernel': kernel, 'bias': bias, 'offset_kernel': offset_kernel, 'offset_bias': offset_bias}
    _L0_conv_all = _L0_conv_setup()
    _L0_conv_in = {k: v for k, v in _L0_conv_all.items() if k in ('kernel', 'bias', 'offset_kernel', 'offset_bias', )}
    del _L0_conv_all

    def _L0_ffn_setup():
        import jax, jax.numpy as jnp
        import numpy as np
        NUM_EXPERTS = 8
        TOP_K = 2
        B, S, D = (8, 8192, 256)

        def _moe(tokens, router_w, w1, b1, w2, b2):
            N = tokens.shape[0]
            E = router_w.shape[0]
            logits = tokens.astype(jnp.float32) @ router_w.astype(jnp.float32).T
            probs = jax.nn.softmax(logits, axis=-1)
            rw, re = jax.lax.top_k(probs, TOP_K)
            if TOP_K > 1:
                rw = rw / jnp.maximum(rw.sum(-1, keepdims=True), 1e-12)
            rw = rw.astype(tokens.dtype)
            combine = jnp.zeros((N, E), tokens.dtype).at[jnp.arange(N)[:, None], re].set(rw)
            out = tokens
            for e in range(E):
                h = jax.nn.gelu(tokens @ w1[e] + b1[e], approximate=False)
                y = h @ w2[e] + b2[e]
                out = out + combine[:, e:e + 1] * y
            return out
        key = jax.random.key(seed)
        ks = jax.random.split(key, 4)
        scale = 1.0 / np.sqrt(D).astype(np.float32)
        return {'input_embeddings': jax.random.normal(ks[0], (B, S, D), jnp.float32), 'router_w': jax.random.normal(ks[1], (NUM_EXPERTS, D), jnp.float32) * scale, 'w1': jax.random.normal(ks[2], (NUM_EXPERTS, D, D), jnp.float32) * scale, 'b1': jnp.zeros((NUM_EXPERTS, D), jnp.float32), 'w2': jax.random.normal(ks[3], (NUM_EXPERTS, D, D), jnp.float32) * scale, 'b2': jnp.zeros((NUM_EXPERTS, D), jnp.float32)}
    _L0_ffn_all = _L0_ffn_setup()
    _L0_ffn_in = {k: v for k, v in _L0_ffn_all.items() if k in ('router_w', 'w1', 'b1', 'w2', 'b2', )}
    del _L0_ffn_all

    return {
        "x": x,
        "L0_conv_kernel": _L0_conv_in["kernel"],
        "L0_conv_bias": _L0_conv_in["bias"],
        "L0_conv_offset_kernel": _L0_conv_in["offset_kernel"],
        "L0_conv_offset_bias": _L0_conv_in["offset_bias"],
        "L0_ffn_router_w": _L0_ffn_in["router_w"],
        "L0_ffn_w1": _L0_ffn_in["w1"],
        "L0_ffn_b1": _L0_ffn_in["b1"],
        "L0_ffn_w2": _L0_ffn_in["w2"],
        "L0_ffn_b2": _L0_ffn_in["b2"],
    }

def reference(x, L0_conv_kernel, L0_conv_bias, L0_conv_offset_kernel, L0_conv_offset_bias, L0_ffn_router_w, L0_ffn_w1, L0_ffn_b1, L0_ffn_w2, L0_ffn_b2):
    import jax
    import jax.numpy as jnp
    def _L0_conv_ref(x, kernel, bias, offset_kernel, offset_bias):
        import jax, jax.numpy as jnp
        import numpy as np
        BS, IH, IW, IC = (4, 64, 64, 256)
        FILTERS = 256
        KH = KW = 3
        KS = KH * KW

        def _dcnv2(x, kernel, bias, offset_kernel, offset_bias):
            bs, ih, iw, ic = x.shape
            kh, kw = (kernel.shape[0], kernel.shape[1])
            ks = kh * kw
            ph, pw = ((kh - 1) // 2, (kw - 1) // 2)
            off = jax.lax.conv_general_dilated(x, offset_kernel, window_strides=(1, 1), padding='SAME', dimension_numbers=('NHWC', 'HWIO', 'NHWC')) + offset_bias
            oyox = off[..., :2 * ks].reshape(bs, ih, iw, ks, 2)
            mask = jax.nn.sigmoid(off[..., 2 * ks:])
            yy, xx = jnp.meshgrid(jnp.arange(-ph, ph + 1), jnp.arange(-pw, pw + 1), indexing='ij')
            patch = jnp.stack([yy, xx], axis=-1).reshape(ks, 2).astype(jnp.float32)
            base = jnp.stack(jnp.meshgrid(jnp.arange(ih), jnp.arange(iw), indexing='ij'), axis=-1).astype(jnp.float32)
            phw = jnp.array([ph, pw], dtype=jnp.float32)
            gyx = base[None, :, :, None, :] + phw + patch + oyox
            bounds = jnp.array([ih + 1, iw + 1], dtype=jnp.float32)
            y0x0 = jnp.floor(gyx)
            y1x1 = jnp.clip(y0x0 + 1.0, 0.0, bounds)
            y0x0 = jnp.clip(y0x0, 0.0, bounds)
            g = jnp.clip(gyx, 0.0, bounds)
            dy0 = g[..., 0] - y0x0[..., 0]
            dx0 = g[..., 1] - y0x0[..., 1]
            dy1 = y1x1[..., 0] - g[..., 0]
            dx1 = y1x1[..., 1] - g[..., 1]
            w = jnp.stack([dy0 * dx0, dy0 * dx1, dy1 * dx0, dy1 * dx1], axis=-1)
            ys = jnp.stack([y1x1[..., 0], y1x1[..., 0], y0x0[..., 0], y0x0[..., 0]], axis=-1).astype(jnp.int32)
            xs = jnp.stack([y1x1[..., 1], y0x0[..., 1], y1x1[..., 1], y0x0[..., 1]], axis=-1).astype(jnp.int32)
            xp = jnp.pad(x, ((0, 0), (ph, ph), (pw, pw), (0, 0)))
            b = jnp.arange(bs)[:, None, None, None, None]
            samples = xp[b, ys, xs]
            bil = jnp.einsum('bhwkg,bhwkgc->bhwkc', w, samples) * mask[..., None]
            map_all = bil.reshape(bs, ih, iw, ks * ic)
            out = jnp.einsum('bhwc,cf->bhwf', map_all, kernel.reshape(ks * ic, -1)) + bias
            return out
        return _dcnv2(x, kernel, bias, offset_kernel, offset_bias)

    def _L0_ffn_ref(input_embeddings, router_w, w1, b1, w2, b2):
        import jax, jax.numpy as jnp
        import numpy as np
        NUM_EXPERTS = 8
        TOP_K = 2
        B, S, D = (8, 8192, 256)

        def _moe(tokens, router_w, w1, b1, w2, b2):
            N = tokens.shape[0]
            E = router_w.shape[0]
            logits = tokens.astype(jnp.float32) @ router_w.astype(jnp.float32).T
            probs = jax.nn.softmax(logits, axis=-1)
            rw, re = jax.lax.top_k(probs, TOP_K)
            if TOP_K > 1:
                rw = rw / jnp.maximum(rw.sum(-1, keepdims=True), 1e-12)
            rw = rw.astype(tokens.dtype)
            combine = jnp.zeros((N, E), tokens.dtype).at[jnp.arange(N)[:, None], re].set(rw)
            out = tokens
            for e in range(E):
                h = jax.nn.gelu(tokens @ w1[e] + b1[e], approximate=False)
                y = h @ w2[e] + b2[e]
                out = out + combine[:, e:e + 1] * y
            return out
        b, s, d = input_embeddings.shape
        tokens = input_embeddings.reshape(b * s, d)
        return _moe(tokens, router_w, w1, b1, w2, b2).reshape(b, s, d)

    def _gn(v, G=32, eps=1e-5):
        B_, H_, W_, C_ = v.shape
        g = v.reshape(B_, H_, W_, G, C_ // G)
        m = jnp.mean(g, axis=(1, 2, 4), keepdims=True)
        s = jnp.var(g, axis=(1, 2, 4), keepdims=True)
        return ((g - m) / jnp.sqrt(s + eps)).reshape(v.shape)

    def _ln_c(v, eps=1e-6):
        m = jnp.mean(v, axis=-1, keepdims=True)
        s = jnp.var(v, axis=-1, keepdims=True)
        return (v - m) / jnp.sqrt(s + eps)

    def _ln_t(v, eps=1e-5):
        m = jnp.mean(v, axis=-1, keepdims=True)
        s = jnp.var(v, axis=-1, keepdims=True)
        return (v - m) / jnp.sqrt(s + eps)

    def _to_tokens(v):
        B_, H_, W_, C_ = v.shape
        return v.reshape(B_, H_ * W_, C_)
    def _from_tokens(t, like):
        return t.reshape(like.shape)

    x = x + _L0_conv_ref(_ln_c(x), L0_conv_kernel, L0_conv_bias, L0_conv_offset_kernel, L0_conv_offset_bias)
    t = _to_tokens(x)
    t = t + _L0_ffn_ref(_ln_t(t), L0_ffn_router_w, L0_ffn_w1, L0_ffn_b1, L0_ffn_w2, L0_ffn_b2)
    x = _from_tokens(t, x)
    return x


_drawn_inputs = setup_inputs


def setup_inputs(seed=0):
    import zlib

    import numpy as np

    out = dict(_drawn_inputs(seed))
    spreads = {'L0_ffn_b1': (0.0, 0.333), 'L0_ffn_b2': (0.0, 0.1)}
    factors = {'L0_conv_offset_bias': 3.844}
    for name, (base, spread) in spreads.items():
        noise = np.random.default_rng([zlib.crc32(name.encode()), seed]).standard_normal(out[name].shape)
        drawn = base * np.exp(spread * noise) if base else spread * noise
        out[name] = jnp.asarray(drawn.astype(out[name].dtype))
    for name, factor in factors.items():
        out[name] = (out[name] * factor).astype(out[name].dtype)
    return out
```

```python
import concourse.bass as bass
from concourse import mybir
from contextlib import ExitStack

BATCH, H, W, C = 4, 64, 64, 256
P = 128
KC = C // P
TAPS, CORNERS = 9, 4
NOFF = 3 * TAPS
NE = 8
TILES = H * W // P
BT = 4
BLOCKS = TILES // BT
SUPERS = BATCH * BLOCKS
PAD = H + 1
XR = 4
PAIRS = 2 * TAPS
UNITS = 2 * PAIRS
RING = 12
GROUPS = UNITS // RING
GP = RING // 2
BILS = 3

ACCS = 2 + NE * BT
ROUTE = 1 + 2 * BT + 2 + 5
MATH = 18

L1_SLOT = [3, 5, 8, 9, 11, 12, 14, 15]
L2_SLOT = [7, 8, 10, 11, 12, 14, 15, 16]
ACC_SLOT = [8, 9, 11, 12, 13, 15, 16, 17]


def lin(i, a, c):
    return i * a + c


def metaformer_kernel(nc, x, wc, cbias, woff, offbias, rwt, w1, b1, w2, b2, ident_c, grid_c, sel_c, iota_c, out):
    fp32, f32r = mybir.dt.float32, mybir.dt.float32r
    i32, u32 = mybir.dt.int32, mybir.dt.uint32
    ALU, ACT = mybir.AluOpType, mybir.ActivationFunctionType

    table = nc.dram_tensor("corner_table", [BATCH * PAD * PAD, CORNERS * C], fp32, kind="Internal").ap()
    table_v = table.rearrange("(b y x) (q c) -> b y x q c", y=PAD, x=PAD, q=CORNERS)
    x_blocks = x.rearrange("b (n r) w c -> (b n) (r w) c", r=2 * BT).rearrange("n (t p) c -> n p t c", p=P)
    out_blocks = out.rearrange("b (n r) w c -> (b n) (r w) c", r=2 * BT).rearrange("n (t p) c -> n p t c", p=P)

    ctx = ExitStack()
    with ctx:
        def sb(name, shape, dt=fp32):
            return ctx.enter_context(nc.sbuf_tensor(name, shape, dt))

        def sem(name):
            return ctx.enter_context(nc.semaphore(name))

        wc_hi, wc_lo = sb("wc_hi", [P, TAPS * KC * C], f32r), sb("wc_lo", [P, TAPS * KC * C], f32r)
        w1_hi, w1_lo = sb("w1_hi", [P, NE * KC * C], f32r), sb("w1_lo", [P, NE * KC * C], f32r)
        w2_sb = sb("w2_sb", [P, NE * KC * C])
        rw_hi, rw_lo = sb("rw_hi", [P, KC, NE], f32r), sb("rw_lo", [P, KC, NE], f32r)
        cb_hi, cb_lo, ones_r = sb("cb_hi", [1, C], f32r), sb("cb_lo", [1, C], f32r), sb("ones_r", [1, P], f32r)
        b1_sb, b2_sb = sb("b1_sb", [P, NE, KC]), sb("b2_sb", [NE, C])
        ident, iota8 = sb("ident", [P, P]), sb("iota8", [P, NE])
        sel, offb = sb("sel", [P, NOFF + 1]), sb("offb", [P, NOFF])
        wall = sb("wall", [P, CORNERS, (SUPERS + 1) * UNITS])
        rows = sb("rows", [P, (SUPERS + 1) * UNITS], i32)
        bt_hi, bt_lo = sb("bt_hi", [P, 2, 4 * P], f32r), sb("bt_lo", [P, 2, 4 * P], f32r)
        ut_hi, ut_lo = sb("ut_hi", [P, KC, BT * P], f32r), sb("ut_lo", [P, KC, BT * P], f32r)
        stats, mv = sb("stats", [P, BT, 6]), sb("mv", [P, BT, 2])
        veps, rstd, mhalf = sb("veps", [P, BT]), sb("rstd", [P, BT]), sb("mhalf", [P, BT])
        imgrow = sb("imgrow", [P, 1])
        rows_st, w_st = sb("rows_st", [P, UNITS], i32), sb("w_st", [P, CORNERS, UNITS])
        logit, top8, topi = sb("logit", [P, BT, NE]), sb("top8", [P, BT, 8]), sb("topi", [P, BT, 8], u32)
        topf, gap, tnh = sb("topf", [P, BT, 2]), sb("gap", [P, BT]), sb("tnh", [P, BT])
        tw, hot, comb = sb("tw", [P, BT, 2]), sb("hot", [P, BT, 2, NE]), sb("comb", [P, BT, NE])
        shared = sb("shared", [P, TILES * 18])
        grid = shared[:, :].rearrange("p (t o) -> p t o", o=18)
        comb_t = shared[0:NE, 0:BT * P]

        PART, XB, OFFS, TMP, MSK = (3 * H * W, XR * BT * C, TILES * NOFF, TILES * 18, TILES * 9)
        b_words = RING * CORNERS * C + BILS * 2 * C + 3 * BT * C + 2 * KC * BT * P
        a_words = PART + XB + OFFS + 3 * TMP + MSK
        arena = sb("arena", [P, max(a_words, b_words)])
        at_word = [0]

        def carve(n):
            at_word[0] += n
            return arena[:, at_word[0] - n:at_word[0]]

        part = carve(PART).rearrange("p (g r) -> p g r", g=3)
        xb = [carve(BT * C).rearrange("p (t c) -> p t c", c=C) for _ in range(XR)]
        off = carve(OFFS).rearrange("p (t o) -> p t o", o=NOFF)
        g = carve(TMP).rearrange("p (t o) -> p t o", o=18)
        t1 = carve(TMP).rearrange("p (t o) -> p t o", o=18)
        gf = carve(TMP).rearrange("p (t o) -> p t o", o=18)
        msk = carve(MSK).rearrange("p (t o) -> p t o", o=9)
        woff_words = KC * 3 * P
        stage_woff = arena[:, PART + XB + OFFS:PART + XB + OFFS + woff_words]
        stage_small = arena[:, PART + XB + OFFS + woff_words:PART + XB + OFFS + woff_words + KC * NE + C]
        at_word[0] = 0
        ring = [carve(CORNERS * C) for _ in range(RING)]
        bil = [carve(2 * C).rearrange("p (t c) -> p t c", c=C) for _ in range(BILS)]
        tok = carve(BT * C).rearrange("p (t c) -> p t c", c=C)
        nrm = carve(BT * C).rearrange("p (t c) -> p t c", c=C)
        acc = carve(BT * C).rearrange("p (t c) -> p t c", c=C)
        hid = [carve(KC * BT * P).rearrange("p (k n) -> p k n", k=KC) for _ in range(2)]

        psum = ctx.enter_context(nc.psum_tensor("psum", [P, 8, 512], fp32))
        woff_hi = bt_hi[:, :, :].rearrange("p a b -> p (a b)")[:, 0:woff_words].rearrange("p (k g m) -> p k g m", k=KC, g=3)
        woff_lo = bt_lo[:, :, :].rearrange("p a b -> p (a b)")[:, 0:woff_words].rearrange("p (k g m) -> p k g m", k=KC, g=3)
        wc_stage = wall[:, :, :].rearrange("p q n -> p (q n)")[:, 0:TAPS * KC * C]

        s_const, s_wc, s_w1, s_w2 = sem("s_const"), sem("s_wc"), sem("s_w1"), sem("s_w2")
        s_zero, s_border, s_setup, s_split = sem("s_zero"), sem("s_border"), sem("s_setup"), sem("s_split")
        s_part0, s_fence, s_half = sem("s_part0"), sem("s_fence"), sem("s_half")
        a_x = [sem(f"a_x{r}") for r in range(XR)]
        a_tab = [sem(f"a_tab{r}") for r in range(XR)]
        a_bst, a_agg, a_eps, a_rstd, a_xn = (sem(n) for n in ("a_bst", "a_agg", "a_eps", "a_rstd", "a_xn"))
        a_tr, a_hi, a_lo, a_part = (sem(n) for n in ("a_tr", "a_hi", "a_lo", "a_part"))
        a_evs, a_evv, a_off, a_offev, a_sig, a_math = (sem(n) for n in ("a_evs", "a_evv", "a_off", "a_offev", "a_sig", "a_math"))
        g_ready = [sem(f"g_ready{r}") for r in range(RING)]
        staged, first_corner, stt, tr, hi_done, lo_done, conv_done = (
            sem(n) for n in ("staged", "first_corner", "stt", "tr", "hi_done", "lo_done", "conv_done"))
        xres, t_done, bst, agg, eps_done, rstd_done, u_done, acc0 = (
            sem(n) for n in ("xres", "t_done", "bst", "agg", "eps_done", "rstd_done", "u_done", "acc0"))
        tu, uthi, utlo, lg, route, tanh_done, ct, cts, b2_done = (
            sem(n) for n in ("tu", "uthi", "utlo", "lg", "route", "tanh_done", "ct", "cts", "b2_done"))
        l1, gelu, l2, acc_done, out_done = (sem(n) for n in ("l1", "gelu", "l2", "acc_done", "out_done"))

        def at(eng, s, value):
            if isinstance(value, int) and value <= 0:
                return
            eng.wait_ge(s, value)

        def at_alone(eng, s, value):
            if isinstance(value, int):
                return at(eng, s, value)
            eng.wait_ge(s, value)
            eng.sem_inc(s_fence, 1)

        def one(a, i):
            if isinstance(i, int):
                return a[i]
            rest = " ".join("abcd"[:len(a.shape) - 2])
            return a[bass.ds(i, 1)].rearrange(f"o p {rest} -> (o p) {rest}")

        def step_items(b, j, lag):
            if isinstance(b, int):
                n = BLOCKS * b + j - lag
                return None if n < 0 or n >= SUPERS else (n // BLOCKS, n % BLOCKS)
            return (b, j - lag) if j >= lag else (b - 1, j - lag + BLOCKS)

        def stage_a(eng, body):
            for j in range(BLOCKS):
                body(0, j)
            with eng.Fori(1, BATCH) as b:
                for j in range(BLOCKS):
                    body(b, j)
            for j in range(4):
                body(BATCH, j)

        def stage_bc(eng, body):
            body(0)
            with eng.Fori(1, SUPERS) as s:
                body(s)
            body(SUPERS)

        def has_conv(s):
            return not (isinstance(s, int) and s >= SUPERS)

        def has_moe(s):
            return not (isinstance(s, int) and s < 1)

        def off_tiles(j):
            return (max(0, BT * j - 1), BT * j + 3 if j < BLOCKS - 1 else TILES)

        def evacuate(eng, n, gi, dx, done):
            bb, jj = n
            dy, sx = gi - 1, dx - 1
            row = 2 * BT * jj - dy
            first, last = max(row, 0), min(row + 2 * BT, H)
            lo_c, hi_c = max(0, sx), W + min(0, sx)
            src = psum[32 * dx:32 * dx + 32, 2 + gi, :].rearrange("p (r w) -> p r w", w=W)[:, first - row:last - row, lo_c:hi_c]
            dst = part[32 * dx:32 * dx + 32, gi, :].rearrange("p (r w) -> p r w", w=W)[:, first:last, lo_c - sx:hi_c - sx]
            if isinstance(bb, int) and bb == 0 and jj == 0:
                eng.wait_ge(s_part0, 1)
            if jj == 0:
                at(eng, a_off, lin(bb, BLOCKS, 0))
            at(eng, a_part, lin(bb, 3 * BLOCKS, 3 * jj + gi + 1))
            if eng is nc.scalar:
                eng.activation(dst, src, ACT.Copy).then_inc(done, 1)
            else:
                eng.tensor_copy(dst, src).then_inc(done, 1)

        block = ctx.enter_context(nc.Block())

        @block.sync
        def _(sp):
            for dst, src in ((ident[:], ident_c), (grid, grid_c), (sel[:], sel_c), (iota8[:], iota_c),
                             (stage_woff, woff), (offb[:], offbias.partition_broadcast(P)),
                             (stage_small[:, 0:KC * NE], rwt), (stage_small[0:1, KC * NE:KC * NE + C], cbias),
                             (b1_sb[:], b1), (b2_sb[:], b2)):
                sp.dma_start(dst, src).then_inc(s_const, 16)

            def body(b, j):
                if (n := step_items(b, j, 0)) is not None:
                    bb, jj = n
                    r = jj % XR
                    at_alone(sp, a_tab[r], lin(bb, 128 * BLOCKS // XR, 128 * (jj // XR)))
                    if isinstance(b, int) and b == 0 and j == XR - 1:
                        sp.wait_ge(s_border, 16 * 6 * BATCH)
                    at_alone(sp, a_tr, lin(bb, BLOCKS, jj - XR + 1))
                    sp.dma_start(xb[r], one(x_blocks, lin(bb, BLOCKS, jj))).then_inc(a_x[r], 16)
                    if isinstance(b, int) and b == 0 and j == 1:
                        sp.dma_start(w2_sb[:], w1).then_inc(s_w1, 16)
                        sp.dma_start(wc_stage, wc).then_inc(s_wc, 16)
                if (n := step_items(b, j, 2)) is not None:
                    bb, jj = n
                    r = jj % XR
                    at_alone(sp, a_xn, lin(bb, BT * BLOCKS, BT * (jj + 1)))
                    for q in range(CORNERS):
                        for half in range(2):
                            y0 = 2 * BT * jj + half + 1 - q // 2
                            x0 = 1 - q % 2
                            dst = one(table_v, bb)[y0:y0 + 2 * BT - 1:2, x0:x0 + W, q, :].rearrange("t x c -> x t c")
                            sp.dma_start(dst, xb[r][half * W:(half + 1) * W, :, :]).then_inc(a_tab[r], 16)

            stage_a(sp, body)
            sp.wait_ge(s_split, 16)
            sp.dma_start(w2_sb[:], w2).then_inc(s_w2, 16)

            def body(s):
                if has_conv(s):
                    if isinstance(s, int) and s == 0:
                        sp.wait_ge(a_math, BATCH * MATH)
                        for r in range(XR):
                            sp.wait_ge(a_tab[r], 128 * SUPERS // XR)
                        sp.dma_start(tok, x_blocks[0]).then_inc(xres, 16)
                    else:
                        at_alone(sp, acc0, s)
                        sp.dma_start(tok, one(x_blocks, s)).then_inc(xres, 16)
                if has_moe(s):
                    at_alone(sp, acc_done, lin(s, ACCS, 0))
                    sp.dma_start(one(out_blocks, s - 1), acc).then_inc(out_done, 16)

            stage_bc(sp, body)
            sp.wait_ge(out_done, 16 * SUPERS)

        @block.gpsimd
        def _(pool):
            pool.memset(mhalf[:], -0.5).then_inc(s_half, 1)
            pool.memset(part[:, :, :], 0.0).then_inc(s_part0, 1)

            def split(hi, lo, src, n, k, parts):
                c = n // parts
                sl = slice(k * c, (k + 1) * c)
                pool.tensor_copy(hi[:, sl], src[:, sl]).then_inc(s_split, 1)
                pool.wait_ge(s_split, 2 * len_done[0] + 1)
                pool.tensor_tensor(out=lo[:, sl], in0=src[:, sl], in1=hi[:, sl].bitcast(fp32), op=ALU.subtract).then_inc(s_split, 1)
                len_done[0] += 1

            len_done = [0]

            def body(b, j):
                if (n := step_items(b, j, 0)) is not None:
                    bb, jj = n
                    at(pool, a_eps, lin(bb, BLOCKS, jj + 1))
                    pool.tensor_tensor(out=rstd[:], in0=veps[:], in1=mhalf[:], op=ALU.pow).then_inc(a_rstd, 1)
                if isinstance(b, int) and b == 0:
                    if j < 4:
                        pool.wait_ge(s_w1, 16)
                        split(w1_hi, w1_lo, w2_sb, NE * KC * C, j, 4)
                    else:
                        pool.wait_ge(s_wc, 16)
                        split(wc_hi, wc_lo, wc_stage, TAPS * KC * C, j - 4, 4)

            pool.wait_ge(s_half, 1)
            stage_a(pool, body)
            pool.wait_ge(s_border, 16 * 6 * BATCH)
            for r in range(XR):
                pool.wait_ge(a_tab[r], 128 * SUPERS // XR)

            def body(s):
                for p in range(PAIRS):
                    if has_conv(s):
                        at_alone(pool, stt, lin(s, 6 * PAIRS, 6 * (p - GP) + 6))
                        if p % GP == 0:
                            at_alone(pool, staged, lin(s, 2 * GROUPS, 2 * (p // GP) + 2))
                        for u in (2 * p, 2 * p + 1):
                            pool.indirect_dma_start(
                                ring[u % RING], None, table,
                                bass.IndirectOffsetOnAxis(ap=rows_st[:, u:u + 1], axis=0)).then_inc(g_ready[u % RING], 16)
                    if has_moe(s):
                        if p == 7:
                            at(pool, eps_done, s)
                            pool.tensor_tensor(out=rstd[:], in0=veps[:], in1=mhalf[:], op=ALU.pow).then_inc(rstd_done, 1)
                        if p == 8:
                            at_alone(pool, u_done, lin(s, BT, 0))
                            at(pool, out_done, lin(s, 16, -16))
                            pool.tensor_tensor(out=acc, in0=tok, in1=nrm, op=ALU.add).then_inc(acc0, 1)

            stage_bc(pool, body)

        @block.scalar
        def _(act):
            act.wait_ge(s_zero, 1)
            z = xb[XR - 1].rearrange("p t c -> p (t c)")
            for b in range(BATCH):
                act.dma_start(table_v[b, 0, :, 0:2, :].rearrange("x q c -> x (q c)"), z[0:PAD, 0:2 * C]).then_inc(s_border, 16)
                act.dma_start(table_v[b, PAD - 1, :, 2:4, :].rearrange("x q c -> x (q c)"), z[0:PAD, 0:2 * C]).then_inc(s_border, 16)
                for x0, q, y0 in ((0, 0, 1), (0, 2, 0), (PAD - 1, 1, 1), (PAD - 1, 3, 0)):
                    act.dma_start(table_v[b, y0:y0 + H, x0, q, :], z[0:H, 0:C]).then_inc(s_border, 16)

            def body(b, j):
                if (n := step_items(b, j, 1)) is not None:
                    bb, jj = n
                    for k in range(KC):
                        at(act, a_tr, lin(bb, BLOCKS, jj + 1))
                        at(act, a_part, lin(bb, 3 * BLOCKS, 3 * jj))
                        act.activation(ut_hi[:, k, :], psum[:, k, :], ACT.Copy).then_inc(a_hi, 1)
                if (n := step_items(b, j, 2)) is not None:
                    for gi, dx in ((0, 0), (0, 1), (1, 0), (1, 1), (2, 0)):
                        evacuate(act, n, gi, dx, a_evs)
                if j == 3 and not (isinstance(b, int) and b == 0):
                    at(act, a_offev, lin(b, BLOCKS, 0))
                    act.activation(msk, off[:, :, 18:27], ACT.Sigmoid).then_inc(a_sig, 1)

            stage_a(act, body)

            def body(s):
                for p in range(PAIRS):
                    if has_conv(s):
                        for t in range(2):
                            u = 2 * p + t
                            if u % RING == 0:
                                at(act, staged, lin(s, 2 * GROUPS, 2 * (u // RING) + 2))
                            if t == 0:
                                at(act, tr, lin(s, PAIRS, p - BILS + 1))
                            at(act, g_ready[u % RING], lin(s, 16 * GROUPS, 16 * (u // RING) + 16))
                            act.activation(bil[p % BILS][:, t, :], ring[u % RING][:, 0:C], ACT.Copy,
                                           scale=w_st[:, 0, u:u + 1]).then_inc(first_corner, 1)
                    if (p > 0 and has_conv(s)) or (p == 0 and has_moe(s)):
                        pp = (p - 1) % PAIRS
                        at(act, tr, lin(s, PAIRS, p))
                        at(act, conv_done, lin(s, PAIRS, p - 2))
                        act.activation(bt_hi[:, pp % 2, :], psum[:, 2 + pp % 2, :], ACT.Copy).then_inc(hi_done, 1)
                    if has_moe(s):
                        if p == 3:
                            for k in range(KC):
                                at(act, tu, s * 1)
                                act.activation(ut_hi[:, k, :], psum[:, 4 + k, :], ACT.Copy).then_inc(uthi, 1)
                        if p == 4:
                            at(act, route, lin(s, ROUTE, 2 * BT + 3 - ROUTE))
                            act.activation(tnh[:], gap[:], ACT.Tanh, scale=0.5).then_inc(tanh_done, 1)
                        if p == 6:
                            at(act, ct, s * 1)
                            act.activation(comb_t, psum[0:NE, 7, :], ACT.Copy).then_inc(cts, 1)
                        for e in range(NE):
                            if L1_SLOT[e] == p:
                                for m in range(KC):
                                    at(act, l1, lin(s, 2 * NE, 2 * e + m + 1 - 2 * NE))
                                    if e >= 2:
                                        at(act, l2, lin(s, 2 * NE, 2 * (e - 1) - 2 * NE))
                                    act.activation(hid[e % 2][:, m, :], psum[:, 4 + m, :], ACT.Gelu,
                                                   bias=b1_sb[:, e, m:m + 1]).then_inc(gelu, 1)

            stage_bc(act, body)

        @block.vector
        def _(dve):
            dve.memset(xb[XR - 1], 0.0).then_inc(s_zero, 1)
            dve.memset(imgrow[:], 0.0).then_inc(s_setup, 1)
            dve.memset(rows[:, SUPERS * UNITS:], 0).then_inc(s_setup, 1)
            dve.wait_ge(s_const, 160)
            whf = woff_hi.rearrange("p k g m -> p (k g m)")
            wlf = woff_lo.rearrange("p k g m -> p (k g m)")
            dve.tensor_copy(whf, stage_woff).then_inc(s_setup, 1)
            dve.tensor_copy(rw_hi[:].rearrange("p k e -> p (k e)"), stage_small[:, 0:KC * NE]).then_inc(s_setup, 1)
            dve.tensor_copy(cb_hi[:], stage_small[0:1, KC * NE:KC * NE + C]).then_inc(s_setup, 1)
            dve.tensor_copy(ones_r[:], ident[0:1, 0:1].to_broadcast([1, P])).then_inc(s_setup, 1)
            dve.wait_ge(s_setup, 6)
            dve.tensor_tensor(wlf, stage_woff, whf.bitcast(fp32), ALU.subtract).then_inc(s_setup, 1)
            dve.tensor_tensor(rw_lo[:].rearrange("p k e -> p (k e)"), stage_small[:, 0:KC * NE],
                              rw_hi[:].rearrange("p k e -> p (k e)").bitcast(fp32), ALU.subtract).then_inc(s_setup, 1)
            dve.tensor_tensor(cb_lo[:], stage_small[0:1, KC * NE:KC * NE + C], cb_hi[:].bitcast(fp32), ALU.subtract).then_inc(s_setup, 1)
            dve.wait_ge(s_setup, 9)

            def norm_stats(src, ready, base, names):
                i, off_n = base
                s_b, s_a, s_e = names
                for t in range(BT):
                    if ready is not None:
                        at(dve, *ready)
                    dve.bn_stats(out=stats[:, t, :], in_=src[:, t, :]).then_inc(s_b, 1)
                for t in range(BT):
                    at_alone(dve, s_b, lin(i, BT * off_n[0], BT * off_n[1] + t + 1))
                    dve.bn_aggr(out=mv[:, t, :], in_=stats[:, t, :]).then_inc(s_a, 1)
                at(dve, s_a, lin(i, BT * off_n[0], BT * off_n[1] + BT))

            def image_math(bi):
                k = [0]

                def link(ins):
                    k[0] += 1
                    ins.then_inc(a_math, 1)
                    dve.wait_ge(a_math, lin(bi, MATH, k[0]))

                at(dve, a_offev, lin(bi, BLOCKS, BLOCKS))
                link(dve.tensor_tensor(g, off[:, :, 0:18], grid, ALU.add))
                link(dve.tensor_scalar(g, g, 0.0, float(PAD), ALU.max, ALU.min))
                link(dve.tensor_copy(t1.bitcast(i32), g))
                link(dve.tensor_copy(gf, t1.bitcast(i32)))
                link(dve.tensor_tensor(t1, gf, g, ALU.is_gt))
                link(dve.tensor_tensor(gf, gf, t1, ALU.subtract))
                link(dve.tensor_scalar(gf, gf, float(PAD - 1), None, ALU.min))
                link(dve.tensor_tensor(g, g, gf, ALU.subtract))
                link(dve.tensor_scalar(t1, g, -1.0, 1.0, ALU.mult, ALU.add))
                dve.wait_ge(a_sig, lin(bi, 1, 1))
                link(dve.tensor_tensor(g[:, :, 0:9], g[:, :, 0:9], msk, ALU.mult))
                link(dve.tensor_tensor(t1[:, :, 0:9], t1[:, :, 0:9], msk, ALU.mult))
                if isinstance(bi, int):
                    dve.wait_ge(s_split, 16)

                def by_unit(a):
                    return a.rearrange("p (h k t) -> p h k t", k=TAPS, t=2)

                def taps(a):
                    return a.rearrange("p (h t) k -> p h k t", t=2)

                cols = slice(bi * TILES * TAPS, (bi + 1) * TILES * TAPS) if isinstance(bi, int) else bass.ds(bi * (TILES * TAPS), TILES * TAPS)
                ys, xs = (t1[:, :, 0:9], g[:, :, 0:9]), (t1[:, :, 9:18], g[:, :, 9:18])
                for q in range(CORNERS):
                    link(dve.tensor_tensor(by_unit(wall[:, q, cols]), taps(ys[q // 2]), taps(xs[q % 2]), ALU.mult))
                link(dve.scalar_tensor_tensor(out=gf[:, :, 0:9], in0=gf[:, :, 0:9], scalar=float(PAD),
                                              in1=gf[:, :, 9:18], op0=ALU.mult, op1=ALU.add))
                link(dve.tensor_scalar(by_unit(rows[:, cols]), taps(gf[:, :, 0:9]), imgrow[:, 0:1], None, ALU.add))
                link(dve.tensor_scalar(imgrow[:], imgrow[:], float(PAD * PAD), None, ALU.add))
                assert k[0] == MATH

            def body(b, j):
                if (n := step_items(b, j, 0)) is not None:
                    bb, jj = n
                    r = jj % XR
                    norm_stats(xb[r], (a_x[r], lin(bb, 16 * BLOCKS // XR, 16 * (jj // XR) + 16)),
                               (bb, (BLOCKS, jj)), (a_bst, a_agg, a_eps))
                    dve.tensor_scalar(veps[:], mv[:, :, 1], 1e-6, None, ALU.add).then_inc(a_eps, 1)
                if (n := step_items(b, j, 1)) is not None:
                    bb, jj = n
                    for k in range(KC):
                        at(dve, a_hi, lin(bb, KC * BLOCKS, KC * jj + k + 1))
                        dve.tensor_tensor(ut_lo[:, k, :], psum[:, k, :], ut_hi[:, k, :].bitcast(fp32), ALU.subtract).then_inc(a_lo, 1)
                if (n := step_items(b, j, 2)) is not None:
                    for gi, dx in ((0, 2), (1, 2), (2, 1), (2, 2)):
                        evacuate(dve, n, gi, dx, a_evv)
                if (n := step_items(b, j, 4)) is not None:
                    bb, jj = n
                    t0, tn = off_tiles(jj)
                    at(dve, a_off, lin(bb, BLOCKS, jj + 1))
                    src = psum[:, 5 + jj % 2, 0:(tn - t0) * (NOFF + 1)].rearrange("p (t o) -> p t o", o=NOFF + 1)[:, :, 0:NOFF]
                    dve.tensor_tensor(off[:, t0:tn, :], src, offb[:, :].unsqueeze(1).to_broadcast([P, tn - t0, NOFF]), ALU.add).then_inc(a_offev, 1)
                if j == 3 and not (isinstance(b, int) and b == 0):
                    image_math(b - 1)
                if (n := step_items(b, j, 0)) is not None:
                    bb, jj = n
                    r = jj % XR
                    for t in range(BT):
                        at(dve, a_rstd, lin(bb, BLOCKS, jj + 1))
                        dve.tensor_scalar(xb[r][:, t, :], xb[r][:, t, :], mv[:, t, 0:1], rstd[:, t:t + 1],
                                          ALU.subtract, ALU.mult).then_inc(a_xn, 1)

            stage_a(dve, body)
            dve.memset(wall[:, :, SUPERS * UNITS:], 0.0).then_inc(a_math, 1)
            dve.wait_ge(a_math, BATCH * MATH + 1)

            def stage_group(s, gr):
                n0 = lin(s, UNITS, gr * RING)
                cols = slice(n0, n0 + RING) if isinstance(s, int) else bass.ds(n0, RING)
                u = slice(gr * RING, (gr + 1) * RING)
                dve.tensor_copy(rows_st[:, u], rows[:, cols]).then_inc(staged, 1)
                dve.tensor_copy(w_st[:, :, u], wall[:, :, cols]).then_inc(staged, 1)

            def moe_step(s, p):
                m = s - 1
                if p == 1:
                    for h in range(2):
                        at(dve, conv_done, lin(s, PAIRS, 0))
                        at(dve, xres, s * 16)
                        dve.tensor_tensor(tok[:, 2 * h:2 * h + 2, :], psum[:, h, :].rearrange("p (t c) -> p t c", c=C),
                                          tok[:, 2 * h:2 * h + 2, :], ALU.add).then_inc(t_done, 1)
                    norm_stats(tok, (t_done, lin(s, 2, 0)), (m, (1, 0)), (bst, agg, eps_done))
                    dve.tensor_scalar(veps[:], mv[:, :, 1], 1e-5, None, ALU.add).then_inc(eps_done, 1)
                if p == 2:
                    for t in range(BT):
                        at(dve, rstd_done, s * 1)
                        dve.tensor_scalar(nrm[:, t, :], tok[:, t, :], mv[:, t, 0:1], rstd[:, t:t + 1],
                                          ALU.subtract, ALU.mult).then_inc(u_done, 1)
                if p == 3:
                    for k in range(KC):
                        at(dve, uthi, lin(m, KC, k + 1))
                        dve.tensor_tensor(ut_lo[:, k, :], psum[:, 4 + k, :], ut_hi[:, k, :].bitcast(fp32), ALU.subtract).then_inc(utlo, 1)
                if p == 4:
                    at(dve, lg, s * 1)
                    dve.tensor_copy(logit[:].rearrange("p t e -> p (t e)"), psum[:, 6, 0:BT * NE]).then_inc(route, 1)
                    at_alone(dve, route, lin(m, ROUTE, 1))
                    for t in range(BT):
                        dve.max(out=top8[:, t, :], in_=logit[:, t, :]).then_inc(route, 1)
                    at_alone(dve, route, lin(m, ROUTE, BT + 1))
                    for t in range(BT):
                        dve.max_index(out=topi[:, t, :], in_max=top8[:, t, :], in_values=logit[:, t, :]).then_inc(route, 1)
                    dve.tensor_tensor(gap[:], top8[:, :, 0], top8[:, :, 1], ALU.subtract).then_inc(route, 1)
                    at(dve, route, lin(m, ROUTE, 2 * BT + 1))
                    dve.tensor_copy(topf[:], topi[:, :, 0:2]).then_inc(route, 1)
                if p == 5:
                    at(dve, tanh_done, s * 1)
                    dve.tensor_scalar(tw[:, :, 0], tnh[:], 0.5, 0.5, ALU.mult, ALU.add).then_inc(route, 1)
                    dve.tensor_scalar(tw[:, :, 1], tnh[:], -0.5, 0.5, ALU.mult, ALU.add).then_inc(route, 1)
                    at(dve, route, lin(m, ROUTE, 2 * BT + 3))
                    dve.tensor_tensor(hot[:], iota8[:].unsqueeze(1).unsqueeze(1).to_broadcast([P, BT, 2, NE]),
                                      topf[:].unsqueeze(3).to_broadcast([P, BT, 2, NE]), ALU.is_equal).then_inc(route, 1)
                    at(dve, route, lin(m, ROUTE, 2 * BT + 6))
                    dve.tensor_tensor(hot[:], hot[:], tw[:].unsqueeze(3).to_broadcast([P, BT, 2, NE]), ALU.mult).then_inc(route, 1)
                    at(dve, route, lin(m, ROUTE, 2 * BT + 7))
                    dve.tensor_tensor(comb[:], hot[:, :, 0, :], hot[:, :, 1, :], ALU.add).then_inc(route, 1)
                if p == 7:
                    for h in range(2):
                        at(dve, b2_done, s * 1)
                        at(dve, acc0, s * 1)
                        dve.tensor_tensor(acc[:, 2 * h:2 * h + 2, :], psum[:, 6 + h, :].rearrange("p (t c) -> p t c", c=C),
                                          acc[:, 2 * h:2 * h + 2, :], ALU.add).then_inc(acc_done, 1)
                for e in range(NE):
                    if ACC_SLOT[e] == p:
                        at(dve, acc_done, lin(m, ACCS, 2 + BT * e))
                        for t in range(BT):
                            if t % 2 == 0:
                                at(dve, l2, lin(m, 2 * NE, 2 * e + t // 2 + 1))
                            dve.scalar_tensor_tensor(out=acc[:, t, :], in0=psum[:, 6 + t // 2, (t % 2) * C:(t % 2 + 1) * C],
                                                     scalar=comb[:, t, e:e + 1], in1=acc[:, t, :],
                                                     op0=ALU.mult, op1=ALU.add).then_inc(acc_done, 1)

            def body(s):
                for p in range(PAIRS):
                    if has_conv(s):
                        at(dve, first_corner, lin(s, 2 * PAIRS, 2 * p + 2))
                        for q in range(1, CORNERS):
                            for t in range(2):
                                u = 2 * p + t
                                if q > 1:
                                    at(dve, stt, lin(s, 6 * PAIRS, 6 * p + 2 * (q - 2) + t + 1))
                                dst = bil[p % BILS][:, t, :]
                                dve.scalar_tensor_tensor(out=dst, in0=ring[u % RING][:, q * C:(q + 1) * C],
                                                         scalar=w_st[:, q, u:u + 1], in1=dst,
                                                         op0=ALU.mult, op1=ALU.add).then_inc(stt, 1)
                    if (p > 0 and has_conv(s)) or (p == 0 and has_moe(s)):
                        pp = (p - 1) % PAIRS
                        at(dve, hi_done, lin(s, PAIRS, p))
                        dve.tensor_tensor(bt_lo[:, pp % 2, :], psum[:, 2 + pp % 2, :], bt_hi[:, pp % 2, :].bitcast(fp32),
                                          ALU.subtract).then_inc(lo_done, 1)
                    if has_conv(s):
                        if p == 0:
                            stage_group(s, GROUPS - 1)
                        elif p % GP == 0:
                            stage_group(s + 1, p // GP - 1)
                    if has_moe(s):
                        moe_step(s, p)

            stage_group(0, 0)
            stage_group(0, 1)
            stage_bc(dve, body)

        @block.tensor
        def _(pe):
            def product(dst, lhs, rhs, first, last):
                for n, (a, c) in enumerate(((0, 0), (0, 1), (1, 0))):
                    ins = pe.matmul(dst, lhs[a], rhs[c], start=first and n == 0, stop=last and n == 2, skip_group_check=True)
                return ins

            pe.wait_ge(s_setup, 9)

            def body(b, j):
                if (n := step_items(b, j, 3)) is not None:
                    bb, jj = n
                    t0, tn = off_tiles(jj)
                    at(pe, a_evs, lin(bb, 5 * BLOCKS, 5 * (jj + 1)))
                    at(pe, a_evv, lin(bb, 4 * BLOCKS, 4 * (jj + 1)))
                    at(pe, a_offev, lin(bb, BLOCKS, jj - 1))
                    for t in range(t0, tn):
                        dst = psum[:, 5 + jj % 2, (t - t0) * (NOFF + 1):(t - t0 + 1) * (NOFF + 1)]
                        for gi in range(3):
                            ins = pe.matmul(dst, part[:, gi, t * P:(t + 1) * P], sel[:], start=gi == 0, stop=gi == 2)
                    ins.then_inc(a_off, 1)
                if (n := step_items(b, j, 0)) is not None:
                    bb, jj = n
                    r = jj % XR
                    at(pe, a_xn, lin(bb, BT * BLOCKS, BT * (jj + 1)))
                    at(pe, a_lo, lin(bb, KC * BLOCKS, KC * jj))
                    for k in range(KC):
                        for t in range(BT):
                            ins = pe.transpose(psum[:, k, t * P:(t + 1) * P], xb[r][:, t, k * P:(k + 1) * P], ident[:])
                    ins.then_inc(a_tr, 1)
                if (n := step_items(b, j, 1)) is not None:
                    bb, jj = n
                    at(pe, a_lo, lin(bb, KC * BLOCKS, KC * (jj + 1)))
                    at(pe, a_evs, lin(bb, 5 * BLOCKS, 5 * jj))
                    at(pe, a_evv, lin(bb, 4 * BLOCKS, 4 * jj))
                    for gi in range(3):
                        for k in range(KC):
                            ins = product(psum[:, 2 + gi, :], (woff_hi[:, k, gi, :], woff_lo[:, k, gi, :]),
                                          (ut_hi[:, k, :], ut_lo[:, k, :]), k == 0, k == KC - 1)
                        ins.then_inc(a_part, 1)

            stage_a(pe, body)
            pe.wait_ge(s_split, 16)
            pe.wait_ge(s_w2, 16)
            pe.wait_ge(a_math, BATCH * MATH + 1)

            def weight(pair_, tap, k, m=None):
                n = (tap * KC + k) * C
                sl = slice(n, n + C) if m is None else slice(n + m * P, n + (m + 1) * P)
                return tuple(w[:, sl] for w in pair_)

            def conv(s, p):
                h = p // TAPS
                at(pe, lo_done, lin(s, PAIRS, p + 1))
                if p % TAPS == 0:
                    at(pe, t_done, lin(s, 2, 0))
                    for t in range(2):
                        dst = psum[:, h, t * C:(t + 1) * C]
                        pe.matmul(dst, ones_r[:], cb_hi[:], start=t == 0, stop=False, skip_group_check=True)
                        pe.matmul(dst, ones_r[:], cb_lo[:], start=False, stop=False, skip_group_check=True)
                for t in range(2):
                    for k in range(KC):
                        n = k * 2 * P + t * P
                        ins = product(psum[:, h, t * C:(t + 1) * C], (bt_hi[:, p % 2, n:n + P], bt_lo[:, p % 2, n:n + P]),
                                      weight((wc_hi, wc_lo), p % TAPS, k), False, p % TAPS == TAPS - 1 and k == KC - 1 and t == 1)
                ins.then_inc(conv_done, 1)

            def moe_step(s, p):
                m = s - 1
                if p == 2:
                    at(pe, u_done, lin(s, BT, 0))
                    at(pe, gelu, lin(m, 2 * NE, 0))
                    for k in range(KC):
                        for t in range(BT):
                            ins = pe.transpose(psum[:, 4 + k, t * P:(t + 1) * P], nrm[:, t, k * P:(k + 1) * P], ident[:])
                    ins.then_inc(tu, 1)
                if p == 3:
                    at(pe, utlo, lin(s, KC, 0))
                    at(pe, acc_done, lin(m, ACCS, 0))
                    for t in range(BT):
                        for k in range(KC):
                            ts = slice(t * P, (t + 1) * P)
                            ins = product(psum[:, 6, t * NE:(t + 1) * NE], (ut_hi[:, k, ts], ut_lo[:, k, ts]),
                                          (rw_hi[:, k, :], rw_lo[:, k, :]), k == 0, k == KC - 1)
                    ins.then_inc(lg, 1)
                if p == 5:
                    at(pe, route, lin(s, ROUTE, 0))
                    for t in range(BT):
                        ins = pe.matmul(psum[0:NE, 7, t * P:(t + 1) * P], comb[:, t, :], ident[:], start=True, stop=True)
                    ins.then_inc(ct, 1)
                if p == 6:
                    at(pe, cts, s * 1)
                    for t in range(BT):
                        ins = pe.matmul(psum[:, 6 + t // 2, (t % 2) * C:(t % 2 + 1) * C], comb_t[:, t * P:(t + 1) * P], b2_sb[:],
                                        start=True, stop=True)
                    ins.then_inc(b2_done, 1)
                for e in range(NE):
                    if L2_SLOT[e] == p:
                        for h in range(2):
                            if h == 0:
                                at(pe, gelu, lin(m, 2 * NE, 2 * e + 2))
                            at(pe, acc_done, lin(m, ACCS, 2 + BT * (e - 1) + 2 * (h + 1) if e else 2))
                            for t in (2 * h, 2 * h + 1):
                                for k in range(KC):
                                    ins = pe.matmul(psum[:, 6 + h, (t % 2) * C:(t % 2 + 1) * C], hid[e % 2][:, k, t * P:(t + 1) * P],
                                                    weight((w2_sb,), e, k)[0], start=k == 0, stop=k == KC - 1)
                            ins.then_inc(l2, 1)
                for e in range(NE):
                    if L1_SLOT[e] == p:
                        for mm in range(KC):
                            at(pe, gelu, lin(m, 2 * NE, 2 * (e - 1) + mm + 1 if e else 0))
                            for k in range(KC):
                                ins = product(psum[:, 4 + mm, :], weight((w1_hi, w1_lo), e, k, mm),
                                              (ut_hi[:, k, :], ut_lo[:, k, :]), k == 0, k == KC - 1)
                            ins.then_inc(l1, 1)

            def body(s):
                for p in range(PAIRS):
                    if has_conv(s):
                        at(pe, stt, lin(s, 6 * PAIRS, 6 * p + 6))
                        at(pe, lo_done, lin(s, PAIRS, p - 1))
                        for k in range(KC):
                            for t in range(2):
                                n = k * 2 * P + t * P
                                ins = pe.transpose(psum[:, 2 + p % 2, n:n + P], bil[p % BILS][:, t, k * P:(k + 1) * P], ident[:])
                        ins.then_inc(tr, 1)
                    if p > 0 and has_conv(s):
                        conv(s, p - 1)
                    elif p == 0 and has_moe(s):
                        conv(s - 1, PAIRS - 1)
                    if has_moe(s):
                        moe_step(s, p)

            stage_bc(pe, body)


def kernel(x, L0_conv_kernel, L0_conv_bias, L0_conv_offset_kernel, L0_conv_offset_bias, L0_ffn_router_w,
           L0_ffn_w1, L0_ffn_b1, L0_ffn_w2, L0_ffn_b2):
    import numpy as np
    import concourse.bacc as bacc
    from concourse import mybir as mb
    from concourse.bass_utils import run_bass_kernel_spmd

    def by_partition(w):
        w = np.asarray(w).reshape(-1, KC, P, w.shape[-1])
        return np.ascontiguousarray(w.transpose(2, 0, 1, 3)).reshape(P, -1)

    order = [2 * k for k in range(TAPS)] + [2 * k + 1 for k in range(TAPS)] + list(range(2 * TAPS, NOFF))
    woff = np.zeros((P, KC, 3, P), np.float32)
    ok = np.asarray(L0_conv_offset_kernel).reshape(3, 3, KC, P, NOFF)[..., order]
    for dx in range(3):
        woff[:, :, :, 32 * dx:32 * dx + NOFF] = ok[:, dx].transpose(2, 1, 0, 3)
    sel = np.zeros((P, NOFF + 1), np.float32)
    for dx in range(3):
        sel[32 * dx + np.arange(NOFF), np.arange(NOFF)] = 1.0
    pix = np.arange(TILES)[None, :] * P + np.arange(P)[:, None]
    ys = (pix // W)[:, :, None] + 1 + (np.arange(TAPS) // 3 - 1)
    xs = (pix % W)[:, :, None] + 1 + (np.arange(TAPS) % 3 - 1)
    grid = np.concatenate([ys, xs], -1).astype(np.float32)
    arrays = {
        "x": np.asarray(x),
        "wc": by_partition(L0_conv_kernel),
        "cbias": np.asarray(L0_conv_bias).reshape(1, C),
        "woff": woff.reshape(P, -1),
        "offbias": np.asarray(L0_conv_offset_bias)[order],
        "rwt": by_partition(np.asarray(L0_ffn_router_w).T),
        "w1": by_partition(L0_ffn_w1),
        "b1": np.asarray(L0_ffn_b1).reshape(NE, KC, P).transpose(2, 0, 1),
        "w2": by_partition(L0_ffn_w2),
        "b2": np.asarray(L0_ffn_b2),
        "ident": np.eye(P, dtype=np.float32),
        "grid": grid,
        "sel": sel,
        "iota": np.tile(np.arange(NE, dtype=np.float32), (P, 1)),
    }
    nc = bacc.Bacc("TRN2", target_bir_lowering=False, num_devices=1)
    sent, args = {}, []
    for name, a in arrays.items():
        sent[f"in_{name}"] = np.ascontiguousarray(a)
        args.append(nc.dram_tensor(f"in_{name}", a.shape, mb.dt.float32, kind="ExternalInput").ap())
    out = nc.dram_tensor("out", (BATCH, H, W, C), mb.dt.float32, kind="ExternalOutput").ap()
    metaformer_kernel(nc, *args, out)
    return run_bass_kernel_spmd(nc, [sent], core_ids=[0]).results[0]["out"]
```

```python
import concourse.bass as bass
from concourse import mybir
from contextlib import ExitStack

BATCH, H, W, C = 4, 64, 64, 256
P = 128
KC = C // P
TAPS, CORNERS = 9, 4
NOFF = 3 * TAPS
NE = 8
TILES = H * W // P
BT = 4
BLOCKS = TILES // BT
SUPERS = BATCH * BLOCKS
PAD = H + 1
XR = 4
PAIRS = 2 * TAPS
UNITS = 2 * PAIRS
RING = 12
GROUPS = UNITS // RING
GP = RING // 2
BILS = 3
LAG = 2

ACT_PARTS = ((0, 0), (0, 1), (0, 2), (1, 0), (1, 1), (2, 0), (2, 1))
DVE_PARTS = ((1, 2), (2, 2))

ACCS = NE * BT
SETUP = 9
ROUTE = 1 + 2 * BT + 2 + 5
MATH = 18

SUM_SLOT, NORM_SLOT, TURN_SLOT, LOGIT_SLOT, TOP_SLOT, MIX_SLOT = 2, 3, 4, 5, 5, 6
POW_SLOT, START_SLOT = 8, 11
ACT_LAG = 1
L1_SLOT = [5 + 2 * e for e in range(NE)]
L2_SLOT = [6 + 2 * e for e in range(NE)]
ACC_SLOT = [7 + 2 * e for e in range(NE)]


def lin(i, a, c):
    return i * a + c


def metaformer_kernel(nc, x, wc, bias_rows, low_row, woff, offbias, rwt, w1, b1, w2, ident_c, grid_c, sel_c, iota_c, out):
    fp32, f32r = mybir.dt.float32, mybir.dt.float32r
    i32, u32 = mybir.dt.int32, mybir.dt.uint32
    ALU, ACT = mybir.AluOpType, mybir.ActivationFunctionType

    table = nc.dram_tensor("corner_table", [BATCH * PAD * PAD, CORNERS * C], fp32, kind="Internal").ap()
    table_v = table.rearrange("(b y x) (q c) -> b y x q c", y=PAD, x=PAD, q=CORNERS)
    x_blocks = x.rearrange("b (n r) w c -> (b n) (r w) c", r=2 * BT).rearrange("n (t p) c -> n p t c", p=P)
    out_blocks = out.rearrange("b (n r) w c -> (b n) (r w) c", r=2 * BT).rearrange("n (t p) c -> n p t c", p=P)

    ctx = ExitStack()
    with ctx:
        def sb(name, shape, dt=fp32):
            return ctx.enter_context(nc.sbuf_tensor(name, shape, dt))

        def sem(name):
            return ctx.enter_context(nc.semaphore(name))

        wc_hi, wc_lo = sb("wc_hi", [P, TAPS * KC * C], f32r), sb("wc_lo", [P, TAPS * KC * C], f32r)
        w1_hi, w1_lo = sb("w1_hi", [P, NE * KC * C], f32r), sb("w1_lo", [P, NE * KC * C], f32r)
        w2_sb = sb("w2_sb", [P, NE * KC * C])
        rw_hi, rw_lo = sb("rw_hi", [P, KC, NE], f32r), sb("rw_lo", [P, KC, NE], f32r)
        biases, ones_r = sb("biases", [P, 3, C], f32r), sb("ones_r", [P, P], f32r)
        b1_sb, low = sb("b1_sb", [P, NE, KC]), sb("low", [P, 1])
        ident, iota8 = sb("ident", [P, P]), sb("iota8", [P, NE])
        sel, offb = sb("sel", [P, NOFF + 1]), sb("offb", [P, NOFF])
        wall = sb("wall", [P, CORNERS, (SUPERS + 1) * UNITS])
        rows = sb("rows", [P, (SUPERS + 1) * UNITS], i32)
        bt_hi, bt_lo = sb("bt_hi", [P, 2, 4 * P], f32r), sb("bt_lo", [P, 2, 4 * P], f32r)
        ut_hi, ut_lo = sb("ut_hi", [P, KC, BT * P], f32r), sb("ut_lo", [P, KC, BT * P], f32r)
        stats, mv = sb("stats", [P, BT, 6]), sb("mv", [P, BT, 2])
        veps, rstd, mhalf = sb("veps", [P, BT]), sb("rstd", [P, BT]), sb("mhalf", [P, BT])
        imgrow = sb("imgrow", [P, 1])
        rows_st, w_st = sb("rows_st", [P, UNITS], i32), sb("w_st", [P, CORNERS, UNITS])
        logit, top8, topi = sb("logit", [P, BT, NE]), sb("top8", [P, BT, 8]), sb("topi", [P, BT, 8], u32)
        topf, gap, tnh = sb("topf", [P, BT, 2]), sb("gap", [P, BT]), sb("tnh", [P, BT])
        tw, hot, comb = sb("tw", [P, BT, 2]), sb("hot", [P, BT, 2, NE]), sb("comb", [P, BT, NE])
        grid = sb("grid", [P, TILES, 18])

        PART, XB, OFFS, TMP, MSK = (3 * H * W, XR * BT * C, TILES * NOFF, TILES * 18, TILES * 9)
        b_words = RING * CORNERS * C + BILS * 2 * C + 3 * BT * C + 2 * KC * BT * P
        a_words = PART + XB + OFFS + 3 * TMP + MSK
        arena = sb("arena", [P, max(a_words, b_words)])
        at_word = [0]

        def carve(n):
            at_word[0] += n
            return arena[:, at_word[0] - n:at_word[0]]

        part = carve(PART).rearrange("p (g r) -> p g r", g=3)
        xb = [carve(BT * C).rearrange("p (t c) -> p t c", c=C) for _ in range(XR)]
        off = carve(OFFS).rearrange("p (t o) -> p t o", o=NOFF)
        g = carve(TMP).rearrange("p (t o) -> p t o", o=18)
        t1 = carve(TMP).rearrange("p (t o) -> p t o", o=18)
        gf = carve(TMP).rearrange("p (t o) -> p t o", o=18)
        msk = carve(MSK).rearrange("p (t o) -> p t o", o=9)
        woff_words = KC * 3 * P
        stage_woff = arena[:, PART + XB + OFFS:PART + XB + OFFS + woff_words]
        stage_rw = arena[:, PART + XB + OFFS + woff_words:PART + XB + OFFS + woff_words + KC * NE]
        stage_bias = xb[2].rearrange("p t c -> p (t c)")[:, 0:3 * C]
        stage_bias_hi = biases[:, :, :].rearrange("p n c -> p (n c)")
        at_word[0] = 0
        ring = [carve(CORNERS * C) for _ in range(RING)]
        bil = [carve(2 * C).rearrange("p (t c) -> p t c", c=C) for _ in range(BILS)]
        tok = carve(BT * C).rearrange("p (t c) -> p t c", c=C)
        nrm = carve(BT * C).rearrange("p (t c) -> p t c", c=C)
        acc = carve(BT * C).rearrange("p (t c) -> p t c", c=C)
        hid = [carve(KC * BT * P).rearrange("p (k n) -> p k n", k=KC) for _ in range(2)]

        psum = ctx.enter_context(nc.psum_tensor("psum", [P, 8, 512], fp32))
        woff_hi = bt_hi[:, :, :].rearrange("p a b -> p (a b)")[:, 0:woff_words].rearrange("p (k g m) -> p k g m", k=KC, g=3)
        woff_lo = bt_lo[:, :, :].rearrange("p a b -> p (a b)")[:, 0:woff_words].rearrange("p (k g m) -> p k g m", k=KC, g=3)
        wc_stage = wall[:, :, :].rearrange("p q n -> p (q n)")[:, 0:TAPS * KC * C]

        s_const, s_wc, s_w1, s_w2 = sem("s_const"), sem("s_wc"), sem("s_w1"), sem("s_w2")
        s_zero, s_border, s_setup, s_split = sem("s_zero"), sem("s_border"), sem("s_setup"), sem("s_split")
        s_part0, s_fence, s_half = sem("s_part0"), sem("s_fence"), sem("s_half")
        a_x = [sem(f"a_x{r}") for r in range(XR)]
        a_tab = [sem(f"a_tab{r}") for r in range(XR)]
        a_bst, a_agg, a_eps, a_rstd, a_xn = (sem(n) for n in ("a_bst", "a_agg", "a_eps", "a_rstd", "a_xn"))
        a_tr, a_hi, a_lo, a_part = (sem(n) for n in ("a_tr", "a_hi", "a_lo", "a_part"))
        a_evs, a_evv, a_off, a_offev, a_sig, a_math = (sem(n) for n in ("a_evs", "a_evv", "a_off", "a_offev", "a_sig", "a_math"))
        g_ready = [sem(f"g_ready{r}") for r in range(RING)]
        staged, first_corner, stt, tr, hi_done, lo_done, conv_done = (
            sem(n) for n in ("staged", "first_corner", "stt", "tr", "hi_done", "lo_done", "conv_done"))
        xres, t_done, bst, agg, eps_done, rstd_done, u_done, acc0 = (
            sem(n) for n in ("xres", "t_done", "bst", "agg", "eps_done", "rstd_done", "u_done", "acc0"))
        tu, uthi, utlo, lg, route, tanh_done = (sem(n) for n in ("tu", "uthi", "utlo", "lg", "route", "tanh_done"))
        l1, gelu, l2, acc_done, out_done = (sem(n) for n in ("l1", "gelu", "l2", "acc_done", "out_done"))

        def at(eng, s, value):
            if isinstance(value, int) and value <= 0:
                return
            eng.wait_ge(s, value)

        def at_alone(eng, s, value):
            if isinstance(value, int):
                return at(eng, s, value)
            eng.wait_ge(s, value)
            eng.sem_inc(s_fence, 1)

        def one(a, i):
            if isinstance(i, int):
                return a[i]
            rest = " ".join("abcd"[:len(a.shape) - 2])
            return a[bass.ds(i, 1)].rearrange(f"o p {rest} -> (o p) {rest}")

        def step_items(b, j, lag):
            if isinstance(b, int):
                n = BLOCKS * b + j - lag
                return None if n < 0 or n >= SUPERS else (n // BLOCKS, n % BLOCKS)
            return (b, j - lag) if j >= lag else (b - 1, j - lag + BLOCKS)

        def stage_a(eng, body):
            for j in range(BLOCKS):
                body(0, j)
            with eng.Fori(1, BATCH) as b:
                for j in range(BLOCKS):
                    body(b, j)
            for j in range(4):
                body(BATCH, j)

        def stage_bc(eng, body):
            body(0)
            body(1)
            with eng.Fori(2, SUPERS) as s:
                body(s)
            body(SUPERS)
            body(SUPERS + 1)

        def has_conv(s):
            return not isinstance(s, int) or s < SUPERS

        def has_moe(s):
            return not isinstance(s, int) or 1 <= s <= SUPERS

        def experts(s, p, slots):
            return ([(e, s - 1) for e in range(NE) if slots[e] == p and has_moe(s)]
                    + [(e, s - 2) for e in range(NE) if slots[e] == p + PAIRS and not (isinstance(s, int) and s < 2)])

        def has_pair(s, p):
            return has_conv(s) if p >= 0 else has_conv(s - 1) and has_moe(s)

        def off_tiles(j):
            return (max(0, BT * j - 1), BT * j + 3 if j < BLOCKS - 1 else TILES)

        def evacuate(eng, n, gi, dx, done):
            bb, jj = n
            dy, sx = gi - 1, dx - 1
            row = 2 * BT * jj - dy
            first, last = max(row, 0), min(row + 2 * BT, H)
            lo_c, hi_c = max(0, sx), W + min(0, sx)
            src = psum[32 * dx:32 * dx + 32, 2 + gi, :].rearrange("p (r w) -> p r w", w=W)[:, first - row:last - row, lo_c:hi_c]
            dst = part[32 * dx:32 * dx + 32, gi, :].rearrange("p (r w) -> p r w", w=W)[:, first:last, lo_c - sx:hi_c - sx]
            if isinstance(bb, int) and bb == 0 and jj == 0:
                eng.wait_ge(s_part0, 1)
            if jj == 0:
                at(eng, a_off, lin(bb, BLOCKS, 0))
            at(eng, a_part, lin(bb, 3 * BLOCKS, 3 * jj + gi + 1))
            if eng is nc.scalar:
                eng.activation(dst, src, ACT.Copy).then_inc(done, 1)
            else:
                eng.tensor_copy(dst, src).then_inc(done, 1)

        block = ctx.enter_context(nc.Block())

        @block.sync
        def _(sp):
            for dst, src in ((ident[:], ident_c), (grid[:], grid_c), (sel[:], sel_c), (iota8[:], iota_c),
                             (stage_woff, woff), (offb[:], offbias.partition_broadcast(P)),
                             (stage_rw, rwt), (stage_bias, bias_rows), (low[:], low_row), (b1_sb[:], b1)):
                sp.dma_start(dst, src).then_inc(s_const, 16)

            def body(b, j):
                if (n := step_items(b, j, 0)) is not None:
                    bb, jj = n
                    r = jj % XR
                    at_alone(sp, a_tab[r], lin(bb, 128 * BLOCKS // XR, 128 * (jj // XR)))
                    if isinstance(b, int) and b == 0 and j == 2:
                        sp.wait_ge(s_setup, SETUP)
                    if isinstance(b, int) and b == 0 and j == XR - 1:
                        sp.wait_ge(s_border, 16 * 6 * BATCH)
                    at_alone(sp, a_tr, lin(bb, BLOCKS, jj - XR + 1))
                    sp.dma_start(xb[r], one(x_blocks, lin(bb, BLOCKS, jj))).then_inc(a_x[r], 16)
                    if isinstance(b, int) and b == 0 and j == 1:
                        sp.dma_start(w2_sb[:], w1).then_inc(s_w1, 16)
                        sp.dma_start(wc_stage, wc).then_inc(s_wc, 16)
                if (n := step_items(b, j, 2)) is not None:
                    bb, jj = n
                    r = jj % XR
                    at_alone(sp, a_xn, lin(bb, BT * BLOCKS, BT * (jj + 1)))
                    for q in range(CORNERS):
                        for half in range(2):
                            y0 = 2 * BT * jj + half + 1 - q // 2
                            x0 = 1 - q % 2
                            dst = one(table_v, bb)[y0:y0 + 2 * BT - 1:2, x0:x0 + W, q, :].rearrange("t x c -> x t c")
                            sp.dma_start(dst, xb[r][half * W:(half + 1) * W, :, :]).then_inc(a_tab[r], 16)

            stage_a(sp, body)
            sp.wait_ge(s_split, 16)
            sp.dma_start(w2_sb[:], w2).then_inc(s_w2, 16)

            def body(s):
                if not (isinstance(s, int) and s < 2):
                    at_alone(sp, acc_done, lin(s, ACCS, -ACCS))
                    sp.dma_start(one(out_blocks, s - 2), acc).then_inc(out_done, 16)
                if has_conv(s):
                    if isinstance(s, int) and s == 0:
                        sp.wait_ge(a_math, BATCH * MATH)
                        for r in range(XR):
                            sp.wait_ge(a_tab[r], 128 * SUPERS // XR)
                        sp.dma_start(tok, x_blocks[0]).then_inc(xres, 16)
                    else:
                        at_alone(sp, acc0, s)
                        sp.dma_start(tok, one(x_blocks, s)).then_inc(xres, 16)

            stage_bc(sp, body)
            sp.wait_ge(out_done, 16 * SUPERS)

        @block.gpsimd
        def _(pool):
            pool.memset(mhalf[:], -0.5).then_inc(s_half, 1)
            pool.memset(part[:, :, :], 0.0).then_inc(s_part0, 1)

            def split(hi, lo, src, n, k, parts):
                c = n // parts
                sl = slice(k * c, (k + 1) * c)
                pool.tensor_copy(hi[:, sl], src[:, sl]).then_inc(s_split, 1)
                pool.wait_ge(s_split, 2 * pieces[0] + 1)
                pool.tensor_tensor(out=lo[:, sl], in0=src[:, sl], in1=hi[:, sl].bitcast(fp32), op=ALU.subtract).then_inc(s_split, 1)
                pieces[0] += 1

            pieces = [0]

            def body(b, j):
                if (n := step_items(b, j, 0)) is not None:
                    bb, jj = n
                    at(pool, a_eps, lin(bb, BLOCKS, jj + 1))
                    pool.tensor_tensor(out=rstd[:], in0=veps[:], in1=mhalf[:], op=ALU.pow).then_inc(a_rstd, 1)
                if isinstance(b, int) and b == 0:
                    if j < 4:
                        pool.wait_ge(s_w1, 16)
                        split(w1_hi, w1_lo, w2_sb, NE * KC * C, j, 4)
                    else:
                        pool.wait_ge(s_wc, 16)
                        split(wc_hi, wc_lo, wc_stage, TAPS * KC * C, j - 4, 4)

            pool.wait_ge(s_half, 1)
            stage_a(pool, body)
            pool.wait_ge(s_border, 16 * 6 * BATCH)
            for r in range(XR):
                pool.wait_ge(a_tab[r], 128 * SUPERS // XR)

            def body(s):
                for p in range(PAIRS):
                    if has_conv(s):
                        at_alone(pool, stt, lin(s, 6 * PAIRS, 6 * (p - GP) + 6))
                        if p % GP == 0:
                            at_alone(pool, staged, lin(s, 2 * GROUPS, 2 * (p // GP) + 2))
                        for u in (2 * p, 2 * p + 1):
                            pool.indirect_dma_start(
                                ring[u % RING], None, table,
                                bass.IndirectOffsetOnAxis(ap=rows_st[:, u:u + 1], axis=0)).then_inc(g_ready[u % RING], 16)
                    if has_moe(s):
                        if p == POW_SLOT:
                            at(pool, eps_done, s)
                            pool.tensor_tensor(out=rstd[:], in0=veps[:], in1=mhalf[:], op=ALU.pow).then_inc(rstd_done, 1)
                        if p == START_SLOT:
                            at_alone(pool, u_done, lin(s, BT, 0))
                            at(pool, out_done, lin(s, 16, -16))
                            pool.tensor_tensor(out=acc, in0=tok, in1=nrm, op=ALU.add).then_inc(acc0, 1)

            stage_bc(pool, body)

        @block.scalar
        def _(act):
            act.wait_ge(s_zero, 1)
            z = xb[XR - 1].rearrange("p t c -> p (t c)")
            for b in range(BATCH):
                act.dma_start(table_v[b, 0, :, 0:2, :].rearrange("x q c -> x (q c)"), z[0:PAD, 0:2 * C]).then_inc(s_border, 16)
                act.dma_start(table_v[b, PAD - 1, :, 2:4, :].rearrange("x q c -> x (q c)"), z[0:PAD, 0:2 * C]).then_inc(s_border, 16)
                for x0, q, y0 in ((0, 0, 1), (0, 2, 0), (PAD - 1, 1, 1), (PAD - 1, 3, 0)):
                    act.dma_start(table_v[b, y0:y0 + H, x0, q, :], z[0:H, 0:C]).then_inc(s_border, 16)

            def body(b, j):
                if (n := step_items(b, j, 2)) is not None:
                    for gi, dx in ACT_PARTS:
                        evacuate(act, n, gi, dx, a_evs)
                if (n := step_items(b, j, 1)) is not None:
                    bb, jj = n
                    for k in range(KC):
                        at(act, a_tr, lin(bb, BLOCKS, jj + 1))
                        at(act, a_part, lin(bb, 3 * BLOCKS, 3 * jj))
                        act.activation(ut_hi[:, k, :], psum[:, k, :], ACT.Copy).then_inc(a_hi, 1)
                if j == 3 and not (isinstance(b, int) and b == 0):
                    at(act, a_offev, lin(b, BLOCKS, 0))
                    act.activation(msk, off[:, :, 18:27], ACT.Sigmoid).then_inc(a_sig, 1)

            stage_a(act, body)

            def body(s):
                for p in range(PAIRS):
                    if has_conv(s):
                        for t in range(2):
                            u = 2 * p + t
                            if u % RING == 0:
                                at(act, staged, lin(s, 2 * GROUPS, 2 * (u // RING) + 2))
                            if t == 0:
                                at(act, tr, lin(s, PAIRS, p - BILS + 1))
                            at(act, g_ready[u % RING], lin(s, 16 * GROUPS, 16 * (u // RING) + 16))
                            act.activation(bil[p % BILS][:, t, :], ring[u % RING][:, 0:C], ACT.Copy,
                                           scale=w_st[:, 0, u:u + 1]).then_inc(first_corner, 1)
                    q = p - LAG - ACT_LAG
                    if has_pair(s, q):
                        at(act, tr, lin(s, PAIRS, q + 1))
                        at(act, conv_done, lin(s, PAIRS, q - 1))
                        act.activation(bt_hi[:, q % 2, :], psum[:, 2 + q % 2, :], ACT.Copy).then_inc(hi_done, 1)
                    if has_moe(s):
                        if p == TURN_SLOT + ACT_LAG:
                            for k in range(KC):
                                at(act, tu, s * 1)
                                act.activation(ut_hi[:, k, :], psum[:, 4 + k, :], ACT.Copy).then_inc(uthi, 1)
                        if p == TOP_SLOT + ACT_LAG:
                            at(act, route, lin(s, ROUTE, 2 * BT + 3 - ROUTE))
                            act.activation(tnh[:], gap[:], ACT.Tanh, scale=0.5).then_inc(tanh_done, 1)
                    for e, m in experts(s, p, [slot + ACT_LAG for slot in L1_SLOT]):
                        for mm in range(KC):
                            at(act, l1, lin(m, 2 * NE, 2 * e + mm + 1))
                            at(act, l2, lin(m, 2 * NE, 2 * (e - 1)))
                            act.activation(hid[e % 2][:, mm, :], psum[:, 4 + mm, :], ACT.Gelu,
                                           bias=b1_sb[:, e, mm:mm + 1]).then_inc(gelu, 1)

            stage_bc(act, body)

        @block.vector
        def _(dve):
            dve.memset(xb[XR - 1], 0.0).then_inc(s_zero, 1)
            dve.memset(imgrow[:], 0.0).then_inc(s_setup, 1)
            dve.memset(rows[:, SUPERS * UNITS:], 0).then_inc(s_setup, 1)
            dve.wait_ge(s_const, 160)
            whf = woff_hi.rearrange("p k g m -> p (k g m)")
            wlf = woff_lo.rearrange("p k g m -> p (k g m)")
            dve.tensor_copy(whf, stage_woff).then_inc(s_setup, 1)
            rhf, rlf = (w[:].rearrange("p k e -> p (k e)") for w in (rw_hi, rw_lo))
            bf = biases[:].rearrange("p n c -> p (n c)")
            dve.tensor_copy(rhf, stage_rw).then_inc(s_setup, 1)
            dve.tensor_copy(bf, stage_bias).then_inc(s_setup, 1)
            dve.tensor_scalar(ones_r[:], ident[:], 0.0, 1.0, ALU.mult, ALU.add).then_inc(s_setup, 1)
            dve.wait_ge(s_setup, 6)
            dve.tensor_tensor(wlf, stage_woff, whf.bitcast(fp32), ALU.subtract).then_inc(s_setup, 1)
            dve.tensor_tensor(rlf, stage_rw, rhf.bitcast(fp32), ALU.subtract).then_inc(s_setup, 1)
            dve.scalar_tensor_tensor(out=bf, in0=bf.bitcast(fp32), scalar=low[:, 0:1], in1=stage_bias,
                                     op0=ALU.mult, op1=ALU.add).then_inc(s_setup, 1)
            dve.wait_ge(s_setup, SETUP)

            def norm_stats(src, ready, base, names):
                i, off_n = base
                s_b, s_a, s_e = names
                for t in range(BT):
                    if ready is not None:
                        at(dve, *ready)
                    dve.bn_stats(out=stats[:, t, :], in_=src[:, t, :]).then_inc(s_b, 1)
                for t in range(BT):
                    at_alone(dve, s_b, lin(i, BT * off_n[0], BT * off_n[1] + t + 1))
                    dve.bn_aggr(out=mv[:, t, :], in_=stats[:, t, :]).then_inc(s_a, 1)
                at(dve, s_a, lin(i, BT * off_n[0], BT * off_n[1] + BT))

            def image_math(bi):
                k = [0]

                def link(ins):
                    k[0] += 1
                    ins.then_inc(a_math, 1)
                    dve.wait_ge(a_math, lin(bi, MATH, k[0]))

                at(dve, a_offev, lin(bi, BLOCKS, BLOCKS))
                link(dve.tensor_tensor(g, off[:, :, 0:18], grid[:], ALU.add))
                link(dve.tensor_scalar(g, g, 0.0, float(PAD), ALU.max, ALU.min))
                link(dve.tensor_copy(t1.bitcast(i32), g))
                link(dve.tensor_copy(gf, t1.bitcast(i32)))
                link(dve.tensor_tensor(t1, gf, g, ALU.is_gt))
                link(dve.tensor_tensor(gf, gf, t1, ALU.subtract))
                link(dve.tensor_scalar(gf, gf, float(PAD - 1), None, ALU.min))
                link(dve.tensor_tensor(g, g, gf, ALU.subtract))
                link(dve.tensor_scalar(t1, g, -1.0, 1.0, ALU.mult, ALU.add))
                dve.wait_ge(a_sig, lin(bi, 1, 1))
                link(dve.tensor_tensor(g[:, :, 0:9], g[:, :, 0:9], msk, ALU.mult))
                link(dve.tensor_tensor(t1[:, :, 0:9], t1[:, :, 0:9], msk, ALU.mult))
                if isinstance(bi, int):
                    dve.wait_ge(s_split, 16)

                def by_unit(a):
                    return a.rearrange("p (h k t) -> p h k t", k=TAPS, t=2)

                def taps(a):
                    return a.rearrange("p (h t) k -> p h k t", t=2)

                cols = slice(bi * TILES * TAPS, (bi + 1) * TILES * TAPS) if isinstance(bi, int) else bass.ds(bi * (TILES * TAPS), TILES * TAPS)
                ys, xs = (t1[:, :, 0:9], g[:, :, 0:9]), (t1[:, :, 9:18], g[:, :, 9:18])
                for q in range(CORNERS):
                    link(dve.tensor_tensor(by_unit(wall[:, q, cols]), taps(ys[q // 2]), taps(xs[q % 2]), ALU.mult))
                link(dve.scalar_tensor_tensor(out=gf[:, :, 0:9], in0=gf[:, :, 0:9], scalar=float(PAD),
                                              in1=gf[:, :, 9:18], op0=ALU.mult, op1=ALU.add))
                link(dve.tensor_scalar(by_unit(rows[:, cols]), taps(gf[:, :, 0:9]), imgrow[:, 0:1], None, ALU.add))
                link(dve.tensor_scalar(imgrow[:], imgrow[:], float(PAD * PAD), None, ALU.add))
                assert k[0] == MATH

            def body(b, j):
                if (n := step_items(b, j, 3)) is not None:
                    for gi, dx in DVE_PARTS:
                        evacuate(dve, n, gi, dx, a_evv)
                if (n := step_items(b, j, 2)) is not None:
                    bb, jj = n
                    for k in range(KC):
                        at(dve, a_hi, lin(bb, KC * BLOCKS, KC * jj + k + 1))
                        dve.tensor_tensor(ut_lo[:, k, :], psum[:, k, :], ut_hi[:, k, :].bitcast(fp32), ALU.subtract).then_inc(a_lo, 1)
                if (n := step_items(b, j, 1)) is not None:
                    bb, jj = n
                    r = jj % XR
                    for t in range(BT):
                        at(dve, a_rstd, lin(bb, BLOCKS, jj + 1))
                        dve.tensor_scalar(xb[r][:, t, :], xb[r][:, t, :], mv[:, t, 0:1], rstd[:, t:t + 1],
                                          ALU.subtract, ALU.mult).then_inc(a_xn, 1)
                if (n := step_items(b, j, 0)) is not None:
                    bb, jj = n
                    r = jj % XR
                    norm_stats(xb[r], (a_x[r], lin(bb, 16 * BLOCKS // XR, 16 * (jj // XR) + 16)),
                               (bb, (BLOCKS, jj)), (a_bst, a_agg, a_eps))
                    dve.tensor_scalar(veps[:], mv[:, :, 1], 1e-6, None, ALU.add).then_inc(a_eps, 1)
                if (n := step_items(b, j, 4)) is not None:
                    bb, jj = n
                    t0, tn = off_tiles(jj)
                    at(dve, a_off, lin(bb, BLOCKS, jj + 1))
                    src = psum[:, 5 + jj % 2, 0:(tn - t0) * (NOFF + 1)].rearrange("p (t o) -> p t o", o=NOFF + 1)[:, :, 0:NOFF]
                    dve.tensor_tensor(off[:, t0:tn, :], src, offb[:, :].unsqueeze(1).to_broadcast([P, tn - t0, NOFF]), ALU.add).then_inc(a_offev, 1)
                if j == 3 and not (isinstance(b, int) and b == 0):
                    image_math(b - 1)

            stage_a(dve, body)
            dve.memset(wall[:, :, SUPERS * UNITS:], 0.0).then_inc(a_math, 1)
            dve.wait_ge(a_math, BATCH * MATH + 1)

            def stage_group(s, gr):
                n0 = lin(s, UNITS, gr * RING)
                cols = slice(n0, n0 + RING) if isinstance(s, int) else bass.ds(n0, RING)
                u = slice(gr * RING, (gr + 1) * RING)
                dve.tensor_copy(rows_st[:, u], rows[:, cols]).then_inc(staged, 1)
                dve.tensor_copy(w_st[:, :, u], wall[:, :, cols]).then_inc(staged, 1)

            def moe_step(s, p):
                m = s - 1
                if p == SUM_SLOT:
                    norm_stats(tok, (t_done, lin(s, 2, 0)), (m, (1, 0)), (bst, agg, eps_done))
                    dve.tensor_scalar(veps[:], mv[:, :, 1], 1e-5, None, ALU.add).then_inc(eps_done, 1)
                if p == NORM_SLOT:
                    for t in range(BT):
                        at(dve, rstd_done, s * 1)
                        dve.tensor_scalar(nrm[:, t, :], tok[:, t, :], mv[:, t, 0:1], rstd[:, t:t + 1],
                                          ALU.subtract, ALU.mult).then_inc(u_done, 1)
                if p == TURN_SLOT:
                    for k in range(KC):
                        at(dve, uthi, lin(m, KC, k + 1))
                        dve.tensor_tensor(ut_lo[:, k, :], psum[:, 4 + k, :], ut_hi[:, k, :].bitcast(fp32), ALU.subtract).then_inc(utlo, 1)
                if p == TOP_SLOT:
                    at(dve, lg, s * 1)
                    dve.tensor_copy(logit[:].rearrange("p t e -> p (t e)"), psum[:, 6, 0:BT * NE]).then_inc(route, 1)
                    at_alone(dve, route, lin(m, ROUTE, 1))
                    for t in range(BT):
                        dve.max(out=top8[:, t, :], in_=logit[:, t, :]).then_inc(route, 1)
                    at_alone(dve, route, lin(m, ROUTE, BT + 1))
                    for t in range(BT):
                        dve.max_index(out=topi[:, t, :], in_max=top8[:, t, :], in_values=logit[:, t, :]).then_inc(route, 1)
                    dve.tensor_tensor(gap[:], top8[:, :, 0], top8[:, :, 1], ALU.subtract).then_inc(route, 1)
                    at(dve, route, lin(m, ROUTE, 2 * BT + 1))
                    dve.tensor_copy(topf[:], topi[:, :, 0:2]).then_inc(route, 1)
                if p == MIX_SLOT:
                    at(dve, tanh_done, s * 1)
                    dve.tensor_scalar(tw[:, :, 0], tnh[:], 0.5, 0.5, ALU.mult, ALU.add).then_inc(route, 1)
                    dve.tensor_scalar(tw[:, :, 1], tnh[:], -0.5, 0.5, ALU.mult, ALU.add).then_inc(route, 1)
                    at(dve, route, lin(m, ROUTE, 2 * BT + 3))
                    dve.tensor_tensor(hot[:], iota8[:].unsqueeze(1).unsqueeze(1).to_broadcast([P, BT, 2, NE]),
                                      topf[:].unsqueeze(3).to_broadcast([P, BT, 2, NE]), ALU.is_equal).then_inc(route, 1)
                    at(dve, route, lin(m, ROUTE, 2 * BT + 6))
                    dve.tensor_tensor(hot[:], hot[:], tw[:].unsqueeze(3).to_broadcast([P, BT, 2, NE]), ALU.mult).then_inc(route, 1)
                    at(dve, route, lin(m, ROUTE, 2 * BT + 7))
                    dve.tensor_tensor(comb[:], hot[:, :, 0, :], hot[:, :, 1, :], ALU.add).then_inc(route, 1)

            def add_experts(s, p):
                for e, m in experts(s, p, ACC_SLOT):
                    if e == 0:
                        at(dve, acc0, lin(m, 1, 1))
                        at(dve, route, lin(m, ROUTE, ROUTE))
                    else:
                        at(dve, acc_done, lin(m, ACCS, BT * e))
                    for t in range(BT):
                        if t % 2 == 0:
                            at(dve, l2, lin(m, 2 * NE, 2 * e + t // 2 + 1))
                        dve.scalar_tensor_tensor(out=acc[:, t, :], in0=psum[:, 6 + t // 2, (t % 2) * C:(t % 2 + 1) * C],
                                                 scalar=comb[:, t, e:e + 1], in1=acc[:, t, :],
                                                 op0=ALU.mult, op1=ALU.add).then_inc(acc_done, 1)

            def body(s):
                for p in range(PAIRS):
                    if has_moe(s) and p == SUM_SLOT:
                        for h in range(2):
                            at(dve, conv_done, lin(s, PAIRS, 0))
                            at(dve, xres, s * 16)
                            dve.tensor_tensor(tok[:, 2 * h:2 * h + 2, :], psum[:, h, :].rearrange("p (t c) -> p t c", c=C),
                                              tok[:, 2 * h:2 * h + 2, :], ALU.add).then_inc(t_done, 1)
                    if has_conv(s):
                        at(dve, first_corner, lin(s, 2 * PAIRS, 2 * p + 2))
                        for q in range(1, CORNERS):
                            for t in range(2):
                                u = 2 * p + t
                                if q > 1:
                                    at(dve, stt, lin(s, 6 * PAIRS, 6 * p + 2 * (q - 2) + t + 1))
                                dst = bil[p % BILS][:, t, :]
                                dve.scalar_tensor_tensor(out=dst, in0=ring[u % RING][:, q * C:(q + 1) * C],
                                                         scalar=w_st[:, q, u:u + 1], in1=dst,
                                                         op0=ALU.mult, op1=ALU.add).then_inc(stt, 1)
                    if has_pair(s, p - LAG):
                        pp = (p - LAG) % 2
                        at(dve, hi_done, lin(s, PAIRS, p - LAG + 1))
                        dve.tensor_tensor(bt_lo[:, pp, :], psum[:, 2 + pp, :], bt_hi[:, pp, :].bitcast(fp32),
                                          ALU.subtract).then_inc(lo_done, 1)
                    if has_conv(s):
                        if p == 0:
                            stage_group(s, GROUPS - 1)
                        elif p % GP == 0:
                            stage_group(s + 1, p // GP - 1)
                    if has_moe(s):
                        moe_step(s, p)
                    add_experts(s, p)

            stage_group(0, 0)
            stage_group(0, 1)
            stage_bc(dve, body)

        @block.tensor
        def _(pe):
            def product(dst, lhs, rhs, first, last):
                for n, (a, c) in enumerate(((0, 0), (0, 1), (1, 0))):
                    ins = pe.matmul(dst, lhs[a], rhs[c], start=first and n == 0, stop=last and n == 2, skip_group_check=True)
                return ins

            pe.wait_ge(s_setup, SETUP)

            def body(b, j):
                if (n := step_items(b, j, 1)) is not None:
                    bb, jj = n
                    at(pe, a_lo, lin(bb, KC * BLOCKS, KC * (jj + 1)))
                    for gi in range(3):
                        for s, parts in ((a_evs, ACT_PARTS), (a_evv, DVE_PARTS)):
                            before = sum(part_[0] <= gi for part_ in parts) - len(parts)
                            at(pe, s, lin(bb, len(parts) * BLOCKS, len(parts) * jj + before))
                        for k in range(KC):
                            ins = product(psum[:, 2 + gi, :], (woff_hi[:, k, gi, :], woff_lo[:, k, gi, :]),
                                          (ut_hi[:, k, :], ut_lo[:, k, :]), k == 0, k == KC - 1)
                        ins.then_inc(a_part, 1)
                if (n := step_items(b, j, 0)) is not None:
                    bb, jj = n
                    r = jj % XR
                    at(pe, a_xn, lin(bb, BT * BLOCKS, BT * (jj + 1)))
                    at(pe, a_lo, lin(bb, KC * BLOCKS, KC * jj))
                    for k in range(KC):
                        for t in range(BT):
                            ins = pe.transpose(psum[:, k, t * P:(t + 1) * P], xb[r][:, t, k * P:(k + 1) * P], ident[:])
                    ins.then_inc(a_tr, 1)
                if (n := step_items(b, j, 2)) is not None:
                    bb, jj = n
                    t0, tn = off_tiles(jj)
                    at(pe, a_evs, lin(bb, len(ACT_PARTS) * BLOCKS, len(ACT_PARTS) * (jj + 1)))
                    at(pe, a_evv, lin(bb, len(DVE_PARTS) * BLOCKS, len(DVE_PARTS) * (jj + 1)))
                    at(pe, a_offev, lin(bb, BLOCKS, jj - 1))
                    for t in range(t0, tn):
                        dst = psum[:, 5 + jj % 2, (t - t0) * (NOFF + 1):(t - t0 + 1) * (NOFF + 1)]
                        for gi in range(3):
                            ins = pe.matmul(dst, part[:, gi, t * P:(t + 1) * P], sel[:], start=gi == 0, stop=gi == 2)
                    ins.then_inc(a_off, 1)

            stage_a(pe, body)
            pe.wait_ge(s_split, 16)
            pe.wait_ge(s_w2, 16)
            pe.wait_ge(a_math, BATCH * MATH + 1)

            def weight(pair_, tap, k, m=None):
                n = (tap * KC + k) * C
                sl = slice(n, n + C) if m is None else slice(n + m * P, n + (m + 1) * P)
                return tuple(w[:, sl] for w in pair_)

            def bias(dst, j, n):
                pe.matmul(dst.rearrange("p (t c) -> p t c", c=C), ones_r[32 * j:32 * j + 2, :],
                          biases[32 * j:32 * j + 2, n:n + 1, :].to_broadcast([2, 2, C]), start=True, stop=False, skip_group_check=True)

            def conv(s, p):
                h = p // TAPS
                at(pe, lo_done, lin(s, PAIRS, p + 1))
                if p % TAPS == 0:
                    at(pe, t_done, lin(s, 2, 0))
                    bias(psum[:, h, :], 0, 2)
                for t in range(2):
                    for k in range(KC):
                        n = k * 2 * P + t * P
                        ins = product(psum[:, h, t * C:(t + 1) * C], (bt_hi[:, p % 2, n:n + P], bt_lo[:, p % 2, n:n + P]),
                                      weight((wc_hi, wc_lo), p % TAPS, k), False, p % TAPS == TAPS - 1 and k == KC - 1 and t == 1)
                ins.then_inc(conv_done, 1)

            def moe_step(s, p):
                m = s - 1
                if p == TURN_SLOT:
                    at(pe, u_done, lin(s, BT, 0))
                    at(pe, gelu, lin(m, 2 * NE, 0))
                    for k in range(KC):
                        for t in range(BT):
                            ins = pe.transpose(psum[:, 4 + k, t * P:(t + 1) * P], nrm[:, t, k * P:(k + 1) * P], ident[:])
                    ins.then_inc(tu, 1)
                if p == LOGIT_SLOT:
                    at(pe, utlo, lin(s, KC, 0))
                    at(pe, acc_done, lin(m, ACCS, 0))
                    for t in range(BT):
                        for k in range(KC):
                            ts = slice(t * P, (t + 1) * P)
                            ins = product(psum[:, 6, t * NE:(t + 1) * NE], (ut_hi[:, k, ts], ut_lo[:, k, ts]),
                                          (rw_hi[:, k, :], rw_lo[:, k, :]), k == 0, k == KC - 1)
                    ins.then_inc(lg, 1)

            def expert_step(s, p):
                for e, m in experts(s, p, L2_SLOT):
                    for h in range(2):
                        if h == 0:
                            at(pe, gelu, lin(m, 2 * NE, 2 * e + 2))
                        if e > 0:
                            at(pe, acc_done, lin(m, ACCS, BT * (e - 1) + 2 * (h + 1)))
                        elif h == 0:
                            at(pe, route, lin(m, ROUTE, 1))
                        bias(psum[:, 6 + h, :], e % 4, e // 4)
                        for t in (2 * h, 2 * h + 1):
                            for k in range(KC):
                                ins = pe.matmul(psum[:, 6 + h, (t % 2) * C:(t % 2 + 1) * C], hid[e % 2][:, k, t * P:(t + 1) * P],
                                                weight((w2_sb,), e, k)[0], start=False, stop=k == KC - 1, skip_group_check=True)
                        ins.then_inc(l2, 1)
                for e, m in experts(s, p, L1_SLOT):
                    for mm in range(KC):
                        at(pe, gelu, lin(m, 2 * NE, 2 * (e - 1) + mm + 1 if e else 0))
                        for k in range(KC):
                            ins = product(psum[:, 4 + mm, :], weight((w1_hi, w1_lo), e, k, mm),
                                          (ut_hi[:, k, :], ut_lo[:, k, :]), k == 0, k == KC - 1)
                        ins.then_inc(l1, 1)

            def body(s):
                for p in range(PAIRS):
                    if has_moe(s):
                        moe_step(s, p)
                    expert_step(s, p)
                    if has_pair(s, p - LAG):
                        conv(s, p - LAG) if p >= LAG else conv(s - 1, p - LAG + PAIRS)
                    if has_conv(s):
                        at(pe, stt, lin(s, 6 * PAIRS, 6 * p + 6))
                        at(pe, lo_done, lin(s, PAIRS, p - 1))
                        for k in range(KC):
                            for t in range(2):
                                n = k * 2 * P + t * P
                                ins = pe.transpose(psum[:, 2 + p % 2, n:n + P], bil[p % BILS][:, t, k * P:(k + 1) * P], ident[:])
                        ins.then_inc(tr, 1)

            stage_bc(pe, body)


def kernel(x, L0_conv_kernel, L0_conv_bias, L0_conv_offset_kernel, L0_conv_offset_bias, L0_ffn_router_w,
           L0_ffn_w1, L0_ffn_b1, L0_ffn_w2, L0_ffn_b2):
    import numpy as np
    import concourse.bacc as bacc
    from concourse import mybir as mb
    from concourse.bass_utils import run_bass_kernel_spmd

    def by_partition(w):
        w = np.asarray(w).reshape(-1, KC, P, w.shape[-1])
        return np.ascontiguousarray(w.transpose(2, 0, 1, 3)).reshape(P, -1)

    order = [2 * k for k in range(TAPS)] + [2 * k + 1 for k in range(TAPS)] + list(range(2 * TAPS, NOFF))
    woff = np.zeros((P, KC, 3, P), np.float32)
    ok = np.asarray(L0_conv_offset_kernel).reshape(3, 3, KC, P, NOFF)[..., order]
    for dx in range(3):
        woff[:, :, :, 32 * dx:32 * dx + NOFF] = ok[:, dx].transpose(2, 1, 0, 3)
    sel = np.zeros((P, NOFF + 1), np.float32)
    for dx in range(3):
        sel[32 * dx + np.arange(NOFF), np.arange(NOFF)] = 1.0
    bias_rows, low = np.zeros((P, 3, C), np.float32), np.zeros((P, 1), np.float32)
    low[1::32] = -1.0
    for r in range(2):
        bias_rows[r::32, 0] = np.asarray(L0_ffn_b2)[:4]
        bias_rows[r::32, 1] = np.asarray(L0_ffn_b2)[4:]
        bias_rows[r, 2] = np.asarray(L0_conv_bias)
    pix = np.arange(TILES)[None, :] * P + np.arange(P)[:, None]
    ys = (pix // W)[:, :, None] + 1 + (np.arange(TAPS) // 3 - 1)
    xs = (pix % W)[:, :, None] + 1 + (np.arange(TAPS) % 3 - 1)
    grid = np.concatenate([ys, xs], -1).astype(np.float32)
    arrays = {
        "x": np.asarray(x),
        "wc": by_partition(L0_conv_kernel),
        "bias_rows": bias_rows.reshape(P, -1),
        "low": low,
        "woff": woff.reshape(P, -1),
        "offbias": np.asarray(L0_conv_offset_bias)[order],
        "rwt": by_partition(np.asarray(L0_ffn_router_w).T),
        "w1": by_partition(L0_ffn_w1),
        "b1": np.asarray(L0_ffn_b1).reshape(NE, KC, P).transpose(2, 0, 1),
        "w2": by_partition(L0_ffn_w2),
        "ident": np.eye(P, dtype=np.float32),
        "grid": grid,
        "sel": sel,
        "iota": np.tile(np.arange(NE, dtype=np.float32), (P, 1)),
    }
    nc = bacc.Bacc("TRN2", target_bir_lowering=False, num_devices=1)
    sent, args = {}, []
    for name, a in arrays.items():
        sent[f"in_{name}"] = np.ascontiguousarray(a)
        args.append(nc.dram_tensor(f"in_{name}", a.shape, mb.dt.float32, kind="ExternalInput").ap())
    out = nc.dram_tensor("out", (BATCH, H, W, C), mb.dt.float32, kind="ExternalOutput").ap()
    metaformer_kernel(nc, *args, out)
    return run_bass_kernel_spmd(nc, [sent], core_ids=[0]).results[0]["out"]
```

```python
import concourse.bass as bass
from concourse import mybir
from contextlib import ExitStack

BATCH, H, W, C = 4, 64, 64, 256
P = 128
KC = C // P
TAPS, CORNERS = 9, 4
NOFF = 3 * TAPS
NE = 8
TILES = H * W // P
BT = 4
BLOCKS = TILES // BT
SUPERS = BATCH * BLOCKS
PAD = H + 1
XR = 4
PAIRS = 2 * TAPS
UNITS = 2 * PAIRS
RING = 12
USES = UNITS // RING
GP = RING // 2
HU = UNITS // 2
PLAN = (CORNERS + 1) * HU
BILS = 6
TURN_LAG = 1
LAG = TURN_LAG + 2

ACT_PARTS = ((0, 0), (0, 1), (0, 2), (1, 0), (1, 1), (1, 2), (2, 0))
DVE_PARTS = ((2, 1), (2, 2))

ACCS = NE * BT
SETUP = 8
ROUTE = 2 + 2 * BT + 2 + 5
MATH = 20

SUM_SLOT, NORM_SLOT, TURN_SLOT, LOGIT_SLOT, TOP_SLOT, MIX_SLOT = (LAG + n for n in (0, 1, 2, 3, 4, 5))
POW_SLOT, START_SLOT = GP + LAG + 1, GP + LAG + 3
ACT_LAG = 1
L1_SLOT = [LAG + 3 + 2 * e for e in range(NE)]
HLO_SLOT = [GP + LAG + 3 + 2 * e for e in range(NE)]
L2_SLOT = [LAG + 4 + 2 * e for e in range(NE)]
ACC_SLOT = [LAG + 5 + 2 * e for e in range(NE - 1)] + [TURN_SLOT + PAIRS]


def lin(i, a, c):
    return i * a + c


def metaformer_kernel(nc, x, wc, bias_rows, low_row, woff, offbias, rwt, w1, b1, w2, ident_c, grid_c, above_c, sel_c, iota_c, out):
    fp32, f32r = mybir.dt.float32, mybir.dt.float32r
    i32, u32 = mybir.dt.int32, mybir.dt.uint32
    ALU, ACT = mybir.AluOpType, mybir.ActivationFunctionType

    table = nc.dram_tensor("corner_table", [BATCH * PAD * PAD, CORNERS * C], fp32, kind="Internal").ap()
    plans = nc.dram_tensor("plans", [SUPERS, P, 2 * PLAN], fp32, kind="Internal").ap()
    table_v = table.rearrange("(b y x) (q c) -> b y x q c", y=PAD, x=PAD, q=CORNERS)
    x_blocks = x.rearrange("b (n r) w c -> (b n) (r w) c", r=2 * BT).rearrange("n (t p) c -> n p t c", p=P)
    out_blocks = out.rearrange("b (n r) w c -> (b n) (r w) c", r=2 * BT).rearrange("n (t p) c -> n p t c", p=P)

    ctx = ExitStack()
    with ctx:
        def sb(name, shape, dt=fp32):
            return ctx.enter_context(nc.sbuf_tensor(name, shape, dt))

        def sem(name):
            return ctx.enter_context(nc.semaphore(name))

        wc_hi, wc_lo = sb("wc_hi", [P, TAPS * KC * C], f32r), sb("wc_lo", [P, TAPS * KC * C], f32r)
        w1_hi, w1_lo = sb("w1_hi", [P, NE * KC * C], f32r), sb("w1_lo", [P, NE * KC * C], f32r)
        w2_hi, w2_lo = sb("w2_hi", [P, NE * KC * C], f32r), sb("w2_lo", [P, NE * KC * C], f32r)
        rw = sb("rw", [P, KC, 2, NE], f32r)
        biases, ones_r = sb("biases", [P, 3, C], f32r), sb("ones_r", [P, P], f32r)
        b1_sb, low = sb("b1_sb", [P, NE, KC]), sb("low", [P, 1])
        ident, iota8 = sb("ident", [P, P]), sb("iota8", [P, NE])
        shared = sb("shared", [P, 4 * BT * NE])
        sel, offb = shared[:, 0:NOFF + 1], shared[:, NOFF + 1:2 * NOFF + 1]
        grid, above = shared[:, 2 * NOFF + 2:2 * NOFF + 20], shared[:, 2 * NOFF + 20:2 * NOFF + 20 + TILES]
        hot = shared[:, 0:2 * BT * NE].rearrange("p (t n e) -> p t n e", n=2, e=NE)
        comb, logit = (shared[:, n * BT * NE:(n + 1) * BT * NE].rearrange("p (t e) -> p t e", e=NE) for n in (2, 3))
        plan_st = sb("plan_st", [P, 2, CORNERS + 1, HU])
        bt_hi, bt_lo = sb("bt_hi", [P, 2, 4 * P], f32r), sb("bt_lo", [P, 2, 4 * P], f32r)
        ut_hi, ut_lo = sb("ut_hi", [P, KC, BT * P], f32r), sb("ut_lo", [P, KC, BT * P], f32r)
        stats, mv = sb("stats", [P, BT, 6]), sb("mv", [P, BT, 2])
        veps, rstd, mhalf = sb("veps", [P, BT]), sb("rstd", [P, BT]), sb("mhalf", [P, BT])
        imgrow = sb("imgrow", [P, 1])
        top8, topi = sb("top8", [P, BT, 8]), sb("topi", [P, BT, 8], u32)
        topf, gap, tnh = sb("topf", [P, BT, 2]), sb("gap", [P, BT]), sb("tnh", [P, BT])
        tw = sb("tw", [P, BT, 2])
        hid_hi, hid_lo = sb("hid_hi", [P, KC, BT * P], f32r), sb("hid_lo", [P, KC, BT * P], f32r)

        PART, XB, OFFS, TMP = (3 * H * W, XR * BT * C, TILES * NOFF, TILES * 18)
        b_words = RING * CORNERS * C + BILS * 2 * C + 3 * BT * C + KC * BT * P
        a_words = PART + XB + OFFS + 2 * TMP + BLOCKS * 2 * PLAN
        arena = sb("arena", [P, max(a_words, b_words)])
        at_word = [0]

        def carve(n):
            at_word[0] += n
            return arena[:, at_word[0] - n:at_word[0]]

        part = carve(PART).rearrange("p (g r) -> p g r", g=3)
        xb = [carve(BT * C).rearrange("p (t c) -> p t c", c=C) for _ in range(XR)]
        off = carve(OFFS).rearrange("p (t o) -> p t o", o=NOFF)
        g, msk = off[:, :, 0:18], off[:, :, 18:27]
        t1 = carve(TMP).rearrange("p (t o) -> p t o", o=18)
        gf = carve(TMP).rearrange("p (t o) -> p t o", o=18)
        plan = carve(BLOCKS * 2 * PLAN)
        plan_v = plan.rearrange("p (h q u) -> p h q u", q=CORNERS + 1, u=HU)
        woff_words = KC * 3 * P
        stage_w = (arena[:, PART + XB + OFFS:PART + XB + OFFS + 2 * TMP], plan)
        stage_woff = arena[:, PART + XB + OFFS:PART + XB + OFFS + woff_words]
        stage_rw = arena[:, PART + XB + OFFS + woff_words:PART + XB + OFFS + woff_words + KC * NE].rearrange("p (k e) -> p k e", e=NE)
        stage_bias = xb[2].rearrange("p t c -> p (t c)")[:, 0:3 * C]
        at_word[0] = 0
        ring = [carve(CORNERS * C) for _ in range(RING)]
        bil = [carve(2 * C).rearrange("p (t c) -> p t c", c=C) for _ in range(BILS)]
        tok = carve(BT * C).rearrange("p (t c) -> p t c", c=C)
        nrm = carve(BT * C).rearrange("p (t c) -> p t c", c=C)
        acc = carve(BT * C).rearrange("p (t c) -> p t c", c=C)
        hid = carve(KC * BT * P).rearrange("p (k n) -> p k n", k=KC)

        psum = ctx.enter_context(nc.psum_tensor("psum", [P, 8, 512], fp32))
        woff_hi = bt_hi[:, :, :].rearrange("p a b -> p (a b)")[:, 0:woff_words].rearrange("p (k g m) -> p k g m", k=KC, g=3)
        woff_lo = bt_lo[:, :, :].rearrange("p a b -> p (a b)")[:, 0:woff_words].rearrange("p (k g m) -> p k g m", k=KC, g=3)

        s_const, s_piece = sem("s_const"), [sem(f"s_piece{r}") for r in range(2)]
        plan_out, plan_in = sem("plan_out"), [sem(f"plan_in{h}") for h in range(2)]
        s_zero, s_border, s_setup, s_split = sem("s_zero"), sem("s_border"), sem("s_setup"), sem("s_split")
        s_part0, s_fence, s_half = sem("s_part0"), sem("s_fence"), sem("s_half")
        a_x = [sem(f"a_x{r}") for r in range(XR)]
        a_tab = [sem(f"a_tab{r}") for r in range(XR)]
        a_bst, a_agg, a_eps, a_rstd, a_xn = (sem(n) for n in ("a_bst", "a_agg", "a_eps", "a_rstd", "a_xn"))
        a_tr, a_hi, a_lo, a_part = (sem(n) for n in ("a_tr", "a_hi", "a_lo", "a_part"))
        a_evs, a_evv, a_off, a_offev, a_sig, a_math = (sem(n) for n in ("a_evs", "a_evv", "a_off", "a_offev", "a_sig", "a_math"))
        g_ready = [sem(f"g_ready{r}") for r in range(RING)]
        first_corner, stt, tr, hi_done, lo_done, conv_done = (
            sem(n) for n in ("first_corner", "stt", "tr", "hi_done", "lo_done", "conv_done"))
        xres, t_done, bst, agg, eps_done, rstd_done, u_done, acc0 = (
            sem(n) for n in ("xres", "t_done", "bst", "agg", "eps_done", "rstd_done", "u_done", "acc0"))
        tu, uthi, utlo, lg, route, tanh_done = (sem(n) for n in ("tu", "uthi", "utlo", "lg", "route", "tanh_done"))
        l1, gelu, hlo, l2, acc_done, out_done = (sem(n) for n in ("l1", "gelu", "hlo", "l2", "acc_done", "out_done"))

        def at(eng, s, value):
            if isinstance(value, int) and value <= 0:
                return
            eng.wait_ge(s, value)

        def at_alone(eng, s, value):
            if isinstance(value, int):
                return at(eng, s, value)
            eng.wait_ge(s, value)
            eng.sem_inc(s_fence, 1)

        def one(a, i):
            if isinstance(i, int):
                return a[i]
            rest = " ".join("abcd"[:len(a.shape) - 2])
            return a[bass.ds(i, 1)].rearrange(f"o p {rest} -> (o p) {rest}")

        def step_items(b, j, lag):
            if isinstance(b, int):
                n = BLOCKS * b + j - lag
                return None if n < 0 or n >= SUPERS else (n // BLOCKS, n % BLOCKS)
            return (b, j - lag) if j >= lag else (b - 1, j - lag + BLOCKS)

        def stage_a(eng, body):
            for j in range(BLOCKS):
                body(0, j)
            with eng.Fori(1, BATCH) as b:
                for j in range(BLOCKS):
                    body(b, j)
            for j in range(4):
                body(BATCH, j)

        def stage_bc(eng, body):
            body(0)
            body(1)
            with eng.Fori(2, SUPERS) as s:
                body(s)
            body(SUPERS)
            body(SUPERS + 1)

        def has_conv(s):
            return not isinstance(s, int) or s < SUPERS

        def has_moe(s):
            return not isinstance(s, int) or 1 <= s <= SUPERS

        def experts(s, p, slots):
            return ([(e, s - 1) for e in range(NE) if slots[e] == p and has_moe(s)]
                    + [(e, s - 2) for e in range(NE) if slots[e] == p + PAIRS and not (isinstance(s, int) and s < 2)])

        def has_pair(s, p):
            return has_conv(s) if p >= 0 else has_conv(s - 1) and has_moe(s)

        def off_tiles(j):
            return (max(0, BT * j - 1), BT * j + 3 if j < BLOCKS - 1 else TILES)

        def evacuate(eng, n, gi, dx, done):
            bb, jj = n
            dy, sx = gi - 1, dx - 1
            row = 2 * BT * jj - dy
            first, last = max(row, 0), min(row + 2 * BT, H)
            lo_c, hi_c = max(0, sx), W + min(0, sx)
            src = psum[32 * dx:32 * dx + 32, 2 + gi, :].rearrange("p (r w) -> p r w", w=W)[:, first - row:last - row, lo_c:hi_c]
            dst = part[32 * dx:32 * dx + 32, gi, :].rearrange("p (r w) -> p r w", w=W)[:, first:last, lo_c - sx:hi_c - sx]
            if isinstance(bb, int) and bb == 0 and jj == 0:
                eng.wait_ge(s_part0, 1)
            if jj == 0:
                at(eng, a_off, lin(bb, BLOCKS, 0))
            at(eng, a_part, lin(bb, 3 * BLOCKS, 3 * jj + gi + 1))
            if eng is nc.scalar:
                eng.activation(dst, src, ACT.Copy).then_inc(done, 1)
            else:
                eng.tensor_copy(dst, src).then_inc(done, 1)

        block = ctx.enter_context(nc.Block())

        @block.sync
        def _(sp):
            for dst, src in ((ident[:], ident_c), (grid[:], grid_c), (above[:], above_c), (sel[:], sel_c), (iota8[:], iota_c),
                             (stage_woff, woff), (offb[:], offbias.partition_broadcast(P)),
                             (stage_rw, rwt), (stage_bias, bias_rows), (low[:], low_row), (b1_sb[:], b1)):
                sp.dma_start(dst, src).then_inc(s_const, 16)

            def put_plan(bi):
                at_alone(sp, a_math, lin(bi, MATH, MATH))
                for jj in range(BLOCKS):
                    sp.dma_start(one(plans, lin(bi, BLOCKS, jj)), plan[:, jj * 2 * PLAN:(jj + 1) * 2 * PLAN]).then_inc(plan_out, 16)

            def body(b, j):
                if (n := step_items(b, j, 0)) is not None:
                    bb, jj = n
                    r = jj % XR
                    at_alone(sp, a_tab[r], lin(bb, 128 * BLOCKS // XR, 128 * (jj // XR)))
                    if isinstance(b, int) and b == 0 and j == 2:
                        sp.wait_ge(s_setup, SETUP)
                    if isinstance(b, int) and b == 0 and j == XR - 1:
                        sp.wait_ge(s_border, 16 * 6 * BATCH)
                    at_alone(sp, a_tr, lin(bb, BLOCKS, jj - XR + 1))
                    sp.dma_start(xb[r], one(x_blocks, lin(bb, BLOCKS, jj))).then_inc(a_x[r], 16)
                if j == 5 and not (isinstance(b, int) and b == 0):
                    put_plan(b - 1)
                if (n := step_items(b, j, 2)) is not None:
                    bb, jj = n
                    r = jj % XR
                    at_alone(sp, a_xn, lin(bb, BT * BLOCKS, BT * (jj + 1)))
                    for q in range(CORNERS):
                        for half in range(2):
                            y0 = 2 * BT * jj + half + 1 - q // 2
                            x0 = 1 - q % 2
                            dst = one(table_v, bb)[y0:y0 + 2 * BT - 1:2, x0:x0 + W, q, :].rearrange("t x c -> x t c")
                            sp.dma_start(dst, xb[r][half * W:(half + 1) * W, :, :]).then_inc(a_tab[r], 16)

            stage_a(sp, body)

            def load_plan(s, h):
                sp.dma_start(plan_st[:, h, :, :].rearrange("p q u -> p (q u)"),
                             one(plans, s)[:, h * PLAN:(h + 1) * PLAN]).then_inc(plan_in[h], 16)

            sp.wait_ge(plan_out, 16 * BLOCKS * (BATCH - 1) + 1)
            load_plan(0, 0)
            load_plan(0, 1)
            put_plan(BATCH - 1)
            sp.wait_ge(plan_out, 16 * SUPERS + 1)

            def body(s):
                if has_conv(s) and has_moe(s):
                    for h in range(2):
                        at_alone(sp, stt, lin(s, 6 * PAIRS, 6 * TAPS * (h + 1) - 6 * PAIRS))
                        load_plan(s, h)
                if not (isinstance(s, int) and s < 2):
                    at_alone(sp, acc_done, lin(s, ACCS, -ACCS))
                    sp.dma_start(one(out_blocks, s - 2), acc).then_inc(out_done, 16)
                if has_conv(s):
                    if isinstance(s, int) and s == 0:
                        sp.wait_ge(a_math, BATCH * MATH)
                        for r in range(XR):
                            sp.wait_ge(a_tab[r], 128 * SUPERS // XR)
                        sp.dma_start(tok, x_blocks[0]).then_inc(xres, 16)
                    else:
                        at_alone(sp, acc0, s)
                        sp.dma_start(tok, one(x_blocks, s)).then_inc(xres, 16)

            stage_bc(sp, body)
            sp.wait_ge(out_done, 16 * SUPERS)

        @block.gpsimd
        def _(pool):
            pool.memset(mhalf[:], -0.5).then_inc(s_half, 1)
            pool.memset(part[:, :, :], 0.0).then_inc(s_part0, 1)

            pieces = [(src[:, k * n // 4:(k + 1) * n // 4], hi[:, k * n // 4:(k + 1) * n // 4], lo[:, k * n // 4:(k + 1) * n // 4])
                      for src, hi, lo, n in ((w1, w1_hi, w1_lo, NE * KC * C), (w2, w2_hi, w2_lo, NE * KC * C), (wc, wc_hi, wc_lo, TAPS * KC * C))
                      for k in range(4)]

            def load_piece(n):
                src = pieces[n][0]
                pool.dma_start(stage_w[n % 2][:, 0:src.shape[1]], src).then_inc(s_piece[n % 2], 16)

            def split_piece(n):
                src, hi, lo = pieces[n]
                whole = stage_w[n % 2][:, 0:src.shape[1]]
                pool.wait_ge(s_piece[n % 2], 16 * (n // 2) + 16)
                pool.tensor_copy(hi, whole).then_inc(s_split, 1)
                pool.wait_ge(s_split, 2 * n + 1)
                pool.tensor_tensor(out=lo, in0=whole, in1=hi.bitcast(fp32), op=ALU.subtract).then_inc(s_split, 1)
                pool.wait_ge(s_split, 2 * n + 2)
                if n + 2 < len(pieces):
                    load_piece(n + 2)
                elif n == len(pieces) - 1:
                    pool.memset(plan[:, 0:1], 0.0).then_inc(plan_out, 1)

            def body(b, j):
                if (n := step_items(b, j, 0)) is not None:
                    bb, jj = n
                    at(pool, a_eps, lin(bb, BLOCKS, jj + 1))
                    pool.tensor_tensor(out=rstd[:], in0=veps[:], in1=mhalf[:], op=ALU.pow).then_inc(a_rstd, 1)
                if isinstance(b, int) and b == 0:
                    for n in range(3 * j // 2, 3 * (j + 1) // 2):
                        split_piece(n)

            pool.wait_ge(s_setup, SETUP)
            load_piece(0)
            load_piece(1)
            pool.wait_ge(s_half, 1)
            stage_a(pool, body)
            pool.wait_ge(s_border, 16 * 6 * BATCH)
            for r in range(XR):
                pool.wait_ge(a_tab[r], 128 * SUPERS // XR)
            pool.wait_ge(a_off, SUPERS)

            def body(s):
                for p in range(PAIRS):
                    for e, m in experts(s, p, HLO_SLOT):
                        for mm in range(KC):
                            at(pool, gelu, lin(m, 4 * NE, 4 * e + 2 * mm + 2))
                            pool.tensor_tensor(out=hid_lo[:, mm, :], in0=hid[:, mm, :], in1=hid_hi[:, mm, :].bitcast(fp32),
                                               op=ALU.subtract).then_inc(hlo, 1)
                    if has_moe(s) and p == POW_SLOT:
                        at(pool, eps_done, s)
                        pool.tensor_tensor(out=rstd[:], in0=veps[:], in1=mhalf[:], op=ALU.pow).then_inc(rstd_done, 1)
                    if has_conv(s):
                        at_alone(pool, stt, lin(s, 6 * PAIRS, 6 * (p - GP) + 6))
                        if p % TAPS == 0:
                            at_alone(pool, plan_in[p // TAPS], lin(s, 16, 16))
                        for u in (2 * p, 2 * p + 1):
                            pool.indirect_dma_start(
                                ring[u % RING], None, table,
                                bass.IndirectOffsetOnAxis(ap=plan_st[:, u // HU, CORNERS, u % HU:u % HU + 1].bitcast(i32), axis=0)).then_inc(g_ready[u % RING], 16)
                    if has_moe(s):
                        if p == START_SLOT:
                            at_alone(pool, u_done, lin(s, BT, 0))
                            at(pool, out_done, lin(s, 16, -16))
                            pool.tensor_tensor(out=acc, in0=tok, in1=nrm, op=ALU.add).then_inc(acc0, 1)

            stage_bc(pool, body)

        @block.scalar
        def _(act):
            act.wait_ge(s_zero, 1)
            z = xb[XR - 1].rearrange("p t c -> p (t c)")
            for b in range(BATCH):
                act.dma_start(table_v[b, 0, :, 0:2, :].rearrange("x q c -> x (q c)"), z[0:PAD, 0:2 * C]).then_inc(s_border, 16)
                act.dma_start(table_v[b, PAD - 1, :, 2:4, :].rearrange("x q c -> x (q c)"), z[0:PAD, 0:2 * C]).then_inc(s_border, 16)
                for x0, q, y0 in ((0, 0, 1), (0, 2, 0), (PAD - 1, 1, 1), (PAD - 1, 3, 0)):
                    act.dma_start(table_v[b, y0:y0 + H, x0, q, :], z[0:H, 0:C]).then_inc(s_border, 16)

            def body(b, j):
                if (n := step_items(b, j, 2)) is not None:
                    for gi, dx in ACT_PARTS:
                        evacuate(act, n, gi, dx, a_evs)
                if (n := step_items(b, j, 1)) is not None:
                    bb, jj = n
                    for k in range(KC):
                        at(act, a_tr, lin(bb, BLOCKS, jj + 1))
                        at(act, a_part, lin(bb, 3 * BLOCKS, 3 * jj))
                        act.activation(ut_hi[:, k, :], psum[:, k, :], ACT.Copy).then_inc(a_hi, 1)
                if j == 3 and not (isinstance(b, int) and b == 0):
                    at(act, a_offev, lin(b, BLOCKS, 0))
                    act.activation(msk, off[:, :, 18:27], ACT.Sigmoid).then_inc(a_sig, 1)

            stage_a(act, body)

            def body(s):
                for p in range(PAIRS):
                    if has_conv(s):
                        for t in range(2):
                            u = 2 * p + t
                            if u % HU == 0:
                                at(act, plan_in[u // HU], lin(s, 16, 16))
                            if t == 0:
                                at(act, tr, lin(s, PAIRS, p - BILS + 1))
                            at(act, g_ready[u % RING], lin(s, 16 * USES, 16 * (u // RING) + 16))
                            act.activation(bil[p % BILS][:, t, :], ring[u % RING][:, 0:C], ACT.Copy,
                                           scale=plan_st[:, u // HU, 0, u % HU:u % HU + 1]).then_inc(first_corner, 1)
                    q = p - LAG
                    if has_pair(s, q):
                        at(act, tr, lin(s, PAIRS, q + 1))
                        at(act, conv_done, lin(s, PAIRS, q - 1))
                        act.activation(bt_hi[:, q % 2, :], psum[:, 2 + q % 2, :], ACT.Copy).then_inc(hi_done, 1)
                    if has_moe(s):
                        if p == TURN_SLOT + ACT_LAG:
                            for k in range(KC):
                                at(act, tu, s * 1)
                                act.activation(ut_hi[:, k, :], psum[:, 4 + k, :], ACT.Copy).then_inc(uthi, 1)
                    for e, m in experts(s, p, [slot + ACT_LAG for slot in L1_SLOT]):
                        for mm in range(KC):
                            at(act, l1, lin(m, 2 * NE, 2 * e + mm + 1))
                            at(act, l2, lin(m, 2 * NE, 2 * e))
                            for dst in (hid_hi[:, mm, :], hid[:, mm, :]):
                                act.activation(dst, psum[:, 4 + mm, :], ACT.Gelu, bias=b1_sb[:, e, mm:mm + 1]).then_inc(gelu, 1)
                    if has_moe(s) and p == TOP_SLOT + ACT_LAG:
                        at(act, route, lin(s, ROUTE, 2 * BT + 3 - ROUTE))
                        act.activation(tnh[:], gap[:], ACT.Tanh, scale=0.5).then_inc(tanh_done, 1)

            stage_bc(act, body)

        @block.vector
        def _(dve):
            dve.memset(xb[XR - 1], 0.0).then_inc(s_zero, 1)
            dve.memset(imgrow[:], 0.0).then_inc(s_setup, 1)
            dve.wait_ge(s_const, 16 * 11)
            whf = woff_hi.rearrange("p k g m -> p (k g m)")
            wlf = woff_lo.rearrange("p k g m -> p (k g m)")
            dve.tensor_copy(whf, stage_woff).then_inc(s_setup, 1)
            rhf, rlf = rw[:, :, 0, :], rw[:, :, 1, :]
            bf = biases[:].rearrange("p n c -> p (n c)")
            dve.tensor_copy(rhf, stage_rw).then_inc(s_setup, 1)
            dve.tensor_copy(bf, stage_bias).then_inc(s_setup, 1)
            dve.tensor_scalar(ones_r[:], ident[:], 0.0, 1.0, ALU.mult, ALU.add).then_inc(s_setup, 1)
            dve.wait_ge(s_setup, 5)
            dve.tensor_tensor(wlf, stage_woff, whf.bitcast(fp32), ALU.subtract).then_inc(s_setup, 1)
            dve.tensor_tensor(rlf, stage_rw, rhf.bitcast(fp32), ALU.subtract).then_inc(s_setup, 1)
            dve.scalar_tensor_tensor(out=bf, in0=bf.bitcast(fp32), scalar=low[:, 0:1], in1=stage_bias,
                                     op0=ALU.mult, op1=ALU.add).then_inc(s_setup, 1)
            dve.wait_ge(s_setup, SETUP)

            def norm_stats(src, ready, base, names):
                i, off_n = base
                s_b, s_a, s_e = names
                for t in range(BT):
                    if ready is not None:
                        at(dve, *ready)
                    dve.bn_stats(out=stats[:, t, :], in_=src[:, t, :]).then_inc(s_b, 1)
                for t in range(BT):
                    at_alone(dve, s_b, lin(i, BT * off_n[0], BT * off_n[1] + t + 1))
                    dve.bn_aggr(out=mv[:, t, :], in_=stats[:, t, :]).then_inc(s_a, 1)
                at(dve, s_a, lin(i, BT * off_n[0], BT * off_n[1] + BT))

            def image_math(bi):
                k = [0]

                def link(ins):
                    k[0] += 1
                    ins.then_inc(a_math, 1)
                    dve.wait_ge(a_math, lin(bi, MATH, k[0]))

                at(dve, a_offev, lin(bi, BLOCKS, BLOCKS))
                at(dve, plan_out, lin(bi, 16 * BLOCKS, 1))
                over = [P, TILES, 9]
                link(dve.tensor_tensor(t1[:, :, 0:9], grid[:, 0:9].unsqueeze(1).to_broadcast(over), above[:].unsqueeze(2).to_broadcast(over), ALU.add))
                link(dve.tensor_tensor(g[:, :, 0:9], g[:, :, 0:9], t1[:, :, 0:9], ALU.add))
                link(dve.tensor_tensor(g[:, :, 9:18], g[:, :, 9:18], grid[:, 9:18].unsqueeze(1).to_broadcast(over), ALU.add))
                link(dve.tensor_scalar(g, g, 0.0, float(PAD), ALU.max, ALU.min))
                link(dve.tensor_copy(t1.bitcast(i32), g))
                link(dve.tensor_copy(gf, t1.bitcast(i32)))
                link(dve.tensor_tensor(t1, gf, g, ALU.is_gt))
                link(dve.tensor_tensor(gf, gf, t1, ALU.subtract))
                link(dve.tensor_scalar(gf, gf, float(PAD - 1), None, ALU.min))
                link(dve.tensor_tensor(g, g, gf, ALU.subtract))
                link(dve.tensor_scalar(t1, g, -1.0, 1.0, ALU.mult, ALU.add))
                dve.wait_ge(a_sig, lin(bi, 1, 1))
                link(dve.tensor_tensor(g[:, :, 0:9], g[:, :, 0:9], msk, ALU.mult))
                link(dve.tensor_tensor(t1[:, :, 0:9], t1[:, :, 0:9], msk, ALU.mult))

                def by_unit(q):
                    return plan_v[:, :, q, :].rearrange("p h (k t) -> p h k t", t=2)

                def taps(a):
                    return a.rearrange("p (h t) k -> p h k t", t=2)

                ys, xs = (t1[:, :, 0:9], g[:, :, 0:9]), (t1[:, :, 9:18], g[:, :, 9:18])
                for q in range(CORNERS):
                    link(dve.tensor_tensor(by_unit(q), taps(ys[q // 2]), taps(xs[q % 2]), ALU.mult))
                link(dve.scalar_tensor_tensor(out=gf[:, :, 0:9], in0=gf[:, :, 0:9], scalar=float(PAD),
                                              in1=gf[:, :, 9:18], op0=ALU.mult, op1=ALU.add))
                link(dve.tensor_scalar(by_unit(CORNERS).bitcast(i32), taps(gf[:, :, 0:9]), imgrow[:, 0:1], None, ALU.add))
                link(dve.tensor_scalar(imgrow[:], imgrow[:], float(PAD * PAD), None, ALU.add))
                assert k[0] == MATH

            def body(b, j):
                if (n := step_items(b, j, 3)) is not None:
                    for gi, dx in DVE_PARTS:
                        evacuate(dve, n, gi, dx, a_evv)
                if (n := step_items(b, j, 2)) is not None:
                    bb, jj = n
                    for k in range(KC):
                        at(dve, a_hi, lin(bb, KC * BLOCKS, KC * jj + k + 1))
                        dve.tensor_tensor(ut_lo[:, k, :], psum[:, k, :], ut_hi[:, k, :].bitcast(fp32), ALU.subtract).then_inc(a_lo, 1)
                if (n := step_items(b, j, 1)) is not None:
                    bb, jj = n
                    r = jj % XR
                    for t in range(BT):
                        at(dve, a_rstd, lin(bb, BLOCKS, jj + 1))
                        dve.tensor_scalar(xb[r][:, t, :], xb[r][:, t, :], mv[:, t, 0:1], rstd[:, t:t + 1],
                                          ALU.subtract, ALU.mult).then_inc(a_xn, 1)
                if (n := step_items(b, j, 0)) is not None:
                    bb, jj = n
                    r = jj % XR
                    norm_stats(xb[r], (a_x[r], lin(bb, 16 * BLOCKS // XR, 16 * (jj // XR) + 16)),
                               (bb, (BLOCKS, jj)), (a_bst, a_agg, a_eps))
                    dve.tensor_scalar(veps[:], mv[:, :, 1], 1e-6, None, ALU.add).then_inc(a_eps, 1)
                if (n := step_items(b, j, 4)) is not None:
                    bb, jj = n
                    t0, tn = off_tiles(jj)
                    at(dve, a_off, lin(bb, BLOCKS, jj + 1))
                    src = psum[:, 5 + jj % 2, 0:(tn - t0) * (NOFF + 1)].rearrange("p (t o) -> p t o", o=NOFF + 1)[:, :, 0:NOFF]
                    dve.tensor_tensor(off[:, t0:tn, :], src, offb[:, :].unsqueeze(1).to_broadcast([P, tn - t0, NOFF]), ALU.add).then_inc(a_offev, 1)
                if j == 3 and not (isinstance(b, int) and b == 0):
                    image_math(b - 1)

            stage_a(dve, body)
            dve.wait_ge(a_math, BATCH * MATH)

            def moe_step(s, p):
                m = s - 1
                if p == SUM_SLOT:
                    norm_stats(tok, (t_done, lin(s, 2, 0)), (m, (1, 0)), (bst, agg, eps_done))
                    dve.tensor_scalar(veps[:], mv[:, :, 1], 1e-5, None, ALU.add).then_inc(eps_done, 1)
                if p == NORM_SLOT:
                    for t in range(BT):
                        at(dve, rstd_done, s * 1)
                        dve.tensor_scalar(nrm[:, t, :], tok[:, t, :], mv[:, t, 0:1], rstd[:, t:t + 1],
                                          ALU.subtract, ALU.mult).then_inc(u_done, 1)
                if p == TURN_SLOT:
                    for k in range(KC):
                        at(dve, uthi, lin(m, KC, k + 1))
                        dve.tensor_tensor(ut_lo[:, k, :], psum[:, 4 + k, :], ut_hi[:, k, :].bitcast(fp32), ALU.subtract).then_inc(utlo, 1)
                if p == TOP_SLOT:
                    at(dve, lg, s * 1)
                    parts = psum[:, 6, 0:2 * BT * NE].rearrange("p (t n e) -> p t n e", n=2, e=NE)
                    dve.tensor_copy(logit, parts[:, :, 0, :]).then_inc(route, 1)
                    at(dve, route, lin(m, ROUTE, 1))
                    dve.tensor_tensor(logit, logit, parts[:, :, 1, :], ALU.add).then_inc(route, 1)
                    at_alone(dve, route, lin(m, ROUTE, 2))
                    for t in range(BT):
                        dve.max(out=top8[:, t, :], in_=logit[:, t, :]).then_inc(route, 1)
                    at_alone(dve, route, lin(m, ROUTE, BT + 2))
                    for t in range(BT):
                        dve.max_index(out=topi[:, t, :], in_max=top8[:, t, :], in_values=logit[:, t, :]).then_inc(route, 1)
                    dve.tensor_tensor(gap[:], top8[:, :, 0], top8[:, :, 1], ALU.subtract).then_inc(route, 1)
                    at(dve, route, lin(m, ROUTE, 2 * BT + 2))
                    dve.tensor_copy(topf[:], topi[:, :, 0:2]).then_inc(route, 1)
                if p == MIX_SLOT:
                    at(dve, tanh_done, s * 1)
                    dve.tensor_scalar(tw[:, :, 0], tnh[:], 0.5, 0.5, ALU.mult, ALU.add).then_inc(route, 1)
                    dve.tensor_scalar(tw[:, :, 1], tnh[:], -0.5, 0.5, ALU.mult, ALU.add).then_inc(route, 1)
                    at(dve, route, lin(m, ROUTE, 2 * BT + 4))
                    dve.tensor_tensor(hot[:], iota8[:].unsqueeze(1).unsqueeze(1).to_broadcast([P, BT, 2, NE]),
                                      topf[:].unsqueeze(3).to_broadcast([P, BT, 2, NE]), ALU.is_equal).then_inc(route, 1)
                    at(dve, route, lin(m, ROUTE, 2 * BT + 7))
                    dve.tensor_tensor(hot[:], hot[:], tw[:].unsqueeze(3).to_broadcast([P, BT, 2, NE]), ALU.mult).then_inc(route, 1)
                    at(dve, route, lin(m, ROUTE, 2 * BT + 8))
                    dve.tensor_tensor(comb[:], hot[:, :, 0, :], hot[:, :, 1, :], ALU.add).then_inc(route, 1)

            def add_experts(s, p):
                for e, m in experts(s, p, ACC_SLOT):
                    if e == 0:
                        at(dve, acc0, lin(m, 1, 1))
                        at(dve, route, lin(m, ROUTE, ROUTE))
                    else:
                        at(dve, acc_done, lin(m, ACCS, BT * e))
                    for t in range(BT):
                        if t % 2 == 0:
                            at(dve, l2, lin(m, 2 * NE, 2 * e + t // 2 + 1))
                        dve.scalar_tensor_tensor(out=acc[:, t, :], in0=psum[:, 6 + t // 2, (t % 2) * C:(t % 2 + 1) * C],
                                                 scalar=comb[:, t, e:e + 1], in1=acc[:, t, :],
                                                 op0=ALU.mult, op1=ALU.add).then_inc(acc_done, 1)

            def body(s):
                for p in range(PAIRS):
                    if has_pair(s, p - LAG):
                        pp = (p - LAG) % 2
                        at(dve, hi_done, lin(s, PAIRS, p - LAG + 1))
                        dve.tensor_tensor(bt_lo[:, pp, :], psum[:, 2 + pp, :], bt_hi[:, pp, :].bitcast(fp32),
                                          ALU.subtract).then_inc(lo_done, 1)
                    early = p in (TURN_SLOT, TOP_SLOT, MIX_SLOT)
                    if p == TURN_SLOT:
                        add_experts(s, p)
                    if has_moe(s) and early:
                        moe_step(s, p)
                    if has_conv(s):
                        at(dve, first_corner, lin(s, 2 * PAIRS, 2 * p + 2))
                        for q in range(1, CORNERS):
                            for t in range(2):
                                u = 2 * p + t
                                if q > 1:
                                    at(dve, stt, lin(s, 6 * PAIRS, 6 * p + 2 * (q - 2) + t + 1))
                                dst = bil[p % BILS][:, t, :]
                                dve.scalar_tensor_tensor(out=dst, in0=ring[u % RING][:, q * C:(q + 1) * C],
                                                         scalar=plan_st[:, u // HU, q, u % HU:u % HU + 1], in1=dst,
                                                         op0=ALU.mult, op1=ALU.add).then_inc(stt, 1)
                    if has_moe(s) and p == SUM_SLOT:
                        for h in range(2):
                            at(dve, conv_done, lin(s, PAIRS, 0))
                            at(dve, xres, s * 16)
                            dve.tensor_tensor(tok[:, 2 * h:2 * h + 2, :], psum[:, h, :].rearrange("p (t c) -> p t c", c=C),
                                              tok[:, 2 * h:2 * h + 2, :], ALU.add).then_inc(t_done, 1)
                    if has_moe(s) and not early:
                        moe_step(s, p)
                    if p != TURN_SLOT:
                        add_experts(s, p)

            stage_bc(dve, body)

        @block.tensor
        def _(pe):
            def product(dst, lhs, rhs, first, last):
                for n, (a, c) in enumerate(((0, 0), (0, 1), (1, 0))):
                    ins = pe.matmul(dst, lhs[a], rhs[c], start=first and n == 0, stop=last and n == 2, skip_group_check=True)
                return ins

            pe.wait_ge(s_setup, SETUP)

            def body(b, j):
                if (n := step_items(b, j, 1)) is not None:
                    bb, jj = n
                    at(pe, a_lo, lin(bb, KC * BLOCKS, KC * (jj + 1)))
                    for gi in range(3):
                        for s, parts in ((a_evs, ACT_PARTS), (a_evv, DVE_PARTS)):
                            before = sum(part_[0] <= gi for part_ in parts) - len(parts)
                            at(pe, s, lin(bb, len(parts) * BLOCKS, len(parts) * jj + before))
                        for k in range(KC):
                            ins = product(psum[:, 2 + gi, :], (woff_hi[:, k, gi, :], woff_lo[:, k, gi, :]),
                                          (ut_hi[:, k, :], ut_lo[:, k, :]), k == 0, k == KC - 1)
                        ins.then_inc(a_part, 1)
                if (n := step_items(b, j, 0)) is not None:
                    bb, jj = n
                    r = jj % XR
                    at(pe, a_xn, lin(bb, BT * BLOCKS, BT * (jj + 1)))
                    at(pe, a_lo, lin(bb, KC * BLOCKS, KC * jj))
                    for k in range(KC):
                        for t in range(BT):
                            ins = pe.transpose(psum[:, k, t * P:(t + 1) * P], xb[r][:, t, k * P:(k + 1) * P], ident[:])
                    ins.then_inc(a_tr, 1)
                if (n := step_items(b, j, 2)) is not None:
                    bb, jj = n
                    t0, tn = off_tiles(jj)
                    at(pe, a_evs, lin(bb, len(ACT_PARTS) * BLOCKS, len(ACT_PARTS) * (jj + 1)))
                    at(pe, a_evv, lin(bb, len(DVE_PARTS) * BLOCKS, len(DVE_PARTS) * (jj + 1)))
                    at(pe, a_offev, lin(bb, BLOCKS, jj - 1))
                    for t in range(t0, tn):
                        dst = psum[:, 5 + jj % 2, (t - t0) * (NOFF + 1):(t - t0 + 1) * (NOFF + 1)]
                        for gi in range(3):
                            ins = pe.matmul(dst, part[:, gi, t * P:(t + 1) * P], sel[:], start=gi == 0, stop=gi == 2)
                    ins.then_inc(a_off, 1)

            stage_a(pe, body)
            pe.wait_ge(s_split, 24)
            pe.wait_ge(a_math, BATCH * MATH)

            def weight(pair_, tap, k, m=None):
                n = (tap * KC + k) * C
                sl = slice(n, n + C) if m is None else slice(n + m * P, n + (m + 1) * P)
                return tuple(w[:, sl] for w in pair_)

            def bias(dst, j, n):
                pe.matmul(dst.rearrange("p (t c) -> p t c", c=C), ones_r[32 * j:32 * j + 2, :],
                          biases[32 * j:32 * j + 2, n:n + 1, :].to_broadcast([2, 2, C]), start=True, stop=False, skip_group_check=True)

            def conv(s, p):
                h = p // TAPS
                at(pe, lo_done, lin(s, PAIRS, p + 1))
                if p % TAPS == 0:
                    at(pe, t_done, lin(s, 2, h - 1))
                    bias(psum[:, h, :], 0, 2)
                for t in range(2):
                    for k in range(KC):
                        n = k * 2 * P + t * P
                        ins = product(psum[:, h, t * C:(t + 1) * C], (bt_hi[:, p % 2, n:n + P], bt_lo[:, p % 2, n:n + P]),
                                      weight((wc_hi, wc_lo), p % TAPS, k), False, p % TAPS == TAPS - 1 and k == KC - 1 and t == 1)
                ins.then_inc(conv_done, 1)

            def moe_step(s, p):
                m = s - 1
                if not has_moe(s):
                    return
                if p == TURN_SLOT:
                    at(pe, u_done, lin(s, BT, 0))
                    at(pe, gelu, lin(m, 4 * NE, 0))
                    for k in range(KC):
                        for t in range(BT):
                            ins = pe.transpose(psum[:, 4 + k, t * P:(t + 1) * P], nrm[:, t, k * P:(k + 1) * P], ident[:])
                    ins.then_inc(tu, 1)
                if p == LOGIT_SLOT:
                    at(pe, utlo, lin(s, KC, 0))
                    at(pe, acc_done, lin(m, ACCS, 0))
                    for t in range(BT):
                        for k in range(KC):
                            ts = slice(t * P, (t + 1) * P)
                            pe.matmul(psum[:, 6, 2 * t * NE:2 * (t + 1) * NE], ut_hi[:, k, ts], rw[:, k, :, :].rearrange("p n e -> p (n e)"),
                                      start=k == 0, stop=False, skip_group_check=True)
                            ins = pe.matmul(psum[:, 6, 2 * t * NE:(2 * t + 1) * NE], ut_lo[:, k, ts], rw[:, k, 0, :],
                                            start=False, stop=k == KC - 1, skip_group_check=True)
                    ins.then_inc(lg, 1)

            def expert_out(s, p):
                for e, m in experts(s, p, L2_SLOT):
                    for h in range(2):
                        if h == 0:
                            at(pe, hlo, lin(m, 2 * NE, 2 * e + 2))
                        if e > 0:
                            at(pe, acc_done, lin(m, ACCS, BT * (e - 1) + 2 * (h + 1)))
                        elif h == 0:
                            at(pe, route, lin(m, ROUTE, 2))
                        bias(psum[:, 6 + h, :], e % 4, e // 4)
                        for t in (2 * h, 2 * h + 1):
                            for k in range(KC):
                                ins = product(psum[:, 6 + h, (t % 2) * C:(t % 2 + 1) * C],
                                              [part_[:, k, t * P:(t + 1) * P] for part_ in (hid_hi, hid_lo)],
                                              weight((w2_hi, w2_lo), e, k), False, k == KC - 1)
                        ins.then_inc(l2, 1)

            def expert_in(s, p):
                for e, m in experts(s, p, L1_SLOT):
                    for mm in range(KC):
                        at(pe, gelu, lin(m, 4 * NE, 4 * (e - 1) + 2 * mm + 2 if e else 0))
                        for k in range(KC):
                            ins = product(psum[:, 4 + mm, :], weight((w1_hi, w1_lo), e, k, mm),
                                          (ut_hi[:, k, :], ut_lo[:, k, :]), k == 0, k == KC - 1)
                        ins.then_inc(l1, 1)

            def body(s):
                for p in range(PAIRS):
                    moe_step(s, p)
                    expert_in(s, p)
                    if has_pair(s, p - LAG):
                        conv(s, p - LAG) if p >= LAG else conv(s - 1, p - LAG + PAIRS)
                    expert_out(s, p)
                    q = p - TURN_LAG
                    if has_pair(s, q):
                        at(pe, stt, lin(s, 6 * PAIRS, 6 * q + 6))
                        at(pe, lo_done, lin(s, PAIRS, q - 1))
                        for k in range(KC):
                            for t in range(2):
                                n = k * 2 * P + t * P
                                ins = pe.transpose(psum[:, 2 + q % 2, n:n + P], bil[q % BILS][:, t, k * P:(k + 1) * P], ident[:])
                        ins.then_inc(tr, 1)

            stage_bc(pe, body)


def kernel(x, L0_conv_kernel, L0_conv_bias, L0_conv_offset_kernel, L0_conv_offset_bias, L0_ffn_router_w,
           L0_ffn_w1, L0_ffn_b1, L0_ffn_w2, L0_ffn_b2):
    import numpy as np
    import concourse.bacc as bacc
    from concourse import mybir as mb
    from concourse.bass_utils import run_bass_kernel_spmd

    def by_partition(w):
        w = np.asarray(w).reshape(-1, KC, P, w.shape[-1])
        return np.ascontiguousarray(w.transpose(2, 0, 1, 3)).reshape(P, -1)

    order = [2 * k for k in range(TAPS)] + [2 * k + 1 for k in range(TAPS)] + list(range(2 * TAPS, NOFF))
    woff = np.zeros((P, KC, 3, P), np.float32)
    ok = np.asarray(L0_conv_offset_kernel).reshape(3, 3, KC, P, NOFF)[..., order]
    for dx in range(3):
        woff[:, :, :, 32 * dx:32 * dx + NOFF] = ok[:, dx].transpose(2, 1, 0, 3)
    sel = np.zeros((P, NOFF + 1), np.float32)
    for dx in range(3):
        sel[32 * dx + np.arange(NOFF), np.arange(NOFF)] = 1.0
    bias_rows, low = np.zeros((P, 3, C), np.float32), np.zeros((P, 1), np.float32)
    low[1::32] = -1.0
    for r in range(2):
        bias_rows[r::32, 0] = np.asarray(L0_ffn_b2)[:4]
        bias_rows[r::32, 1] = np.asarray(L0_ffn_b2)[4:]
        bias_rows[r, 2] = np.asarray(L0_conv_bias)
    pix = np.arange(TILES)[None, :] * P + np.arange(P)[:, None]
    ys = (pix // W)[:, :, None] + 1 + (np.arange(TAPS) // 3 - 1)
    xs = (pix % W)[:, :, None] + 1 + (np.arange(TAPS) % 3 - 1)
    grid = np.concatenate([ys, xs], -1).astype(np.float32)[:, 0]
    arrays = {
        "x": np.asarray(x),
        "wc": by_partition(L0_conv_kernel),
        "bias_rows": bias_rows.reshape(P, -1),
        "low": low,
        "woff": woff.reshape(P, -1),
        "offbias": np.asarray(L0_conv_offset_bias)[order],
        "rwt": by_partition(np.asarray(L0_ffn_router_w).T),
        "w1": by_partition(L0_ffn_w1),
        "b1": np.asarray(L0_ffn_b1).reshape(NE, KC, P).transpose(2, 0, 1),
        "w2": by_partition(L0_ffn_w2),
        "ident": np.eye(P, dtype=np.float32),
        "grid": grid,
        "above": np.tile(2.0 * np.arange(TILES, dtype=np.float32), (P, 1)),
        "sel": sel,
        "iota": np.tile(np.arange(NE, dtype=np.float32), (P, 1)),
    }
    nc = bacc.Bacc("TRN2", target_bir_lowering=False, num_devices=1)
    sent, args = {}, []
    for name, a in arrays.items():
        sent[f"in_{name}"] = np.ascontiguousarray(a)
        args.append(nc.dram_tensor(f"in_{name}", a.shape, mb.dt.float32, kind="ExternalInput").ap())
    out = nc.dram_tensor("out", (BATCH, H, W, C), mb.dt.float32, kind="ExternalOutput").ap()
    metaformer_kernel(nc, *args, out)
    return run_bass_kernel_spmd(nc, [sent], core_ids=[0]).results[0]["out"]
```
